# Optimizing a Trainium2 kernel written in Bass

```python
import numpy as np
import jax
import jax.numpy as jnp

def _softmax(x, axis=-1):
    return jax.nn.softmax(x, axis=axis)

def _gelu(x):
    return jax.nn.gelu(x, approximate=True)

def _silu(x):
    return jax.nn.silu(x)

def _sigmoid(x):
    return jax.nn.sigmoid(x)

def _layernorm(x, axis=-1, eps=1e-05):
    m = jnp.mean(x, axis=axis, keepdims=True)
    v = jnp.var(x, axis=axis, keepdims=True)
    return (x - m) / jnp.sqrt(v + eps)

def _scatter_add(tgt, idx, src, axis=0):
    return tgt.at[idx].add(src)

def _segment_sum(src, seg, n):
    return jax.ops.segment_sum(src, seg, n)
kernel_name = 'mk_cond_resid_d4_seqx_r4_4a759b'

def setup_inputs(seed: int=0):
    np.random.seed(seed)
    _w = jnp.asarray

    def _rec_inputs():
        import jax
        import jax.numpy as jnp
        _rk = jax.random.key(seed)
        x = -7.109e-05 + 0.9999 * jax.random.normal(jax.random.fold_in(_rk, 1), (8, 256, 1024), jnp.float32)
        _lenS = 256 - jax.random.randint(jax.random.fold_in(_rk, 7), (8,), 0, max(1, 256 // 4) + 1, jnp.int32)
        _lenS2 = 256 - jax.random.randint(jax.random.fold_in(_rk, 8), (8,), 0, max(1, 256 // 4) + 1, jnp.int32)
        condB_thresholds = jax.random.uniform(jax.random.fold_in(_rk, 11), (8,), jnp.float32, 0.0, 1.82799)
        condB_deltas = jax.random.uniform(jax.random.fold_in(_rk, 12), (8,), jnp.float32, 0.0, 0.0232459)
        condB_zeropoints = jax.random.uniform(jax.random.fold_in(_rk, 13), (8,), jnp.float32, 0.0, 243)
        itok_B_3_7 = jax.random.randint(jax.random.fold_in(_rk, 14), (8,), 3, 8, jnp.int32)
        itok_B_0_2 = jax.random.randint(jax.random.fold_in(_rk, 15), (8,), 0, 3, jnp.int32)
        return (x, condB_thresholds, condB_deltas, condB_zeropoints, itok_B_3_7, itok_B_0_2)
    x, condB_thresholds, condB_deltas, condB_zeropoints, itok_B_3_7, itok_B_0_2 = _rec_inputs()

    def _L0_cond_setup():
        import jax, jax.numpy as jnp
        import numpy as np
        N_LEVELS = 64
        key = jax.random.key(seed)
        k1, k2, k3, k4 = jax.random.split(key, 4)
        x = jax.random.normal(k1, (4, 1024, 1024), dtype=jnp.float32)
        G = 4
        thresholds = jnp.sort(jax.random.uniform(k2, (G,), minval=0.2, maxval=3.0))[::-1].astype(jnp.float32)
        deltas = (jax.random.uniform(k3, (G,)) * 0.02 + 0.005).astype(jnp.float32)
        zero_points = jnp.round(jax.random.uniform(k4, (G,)) * (N_LEVELS - 1)).astype(jnp.float32)
        return {'x': x, 'thresholds': thresholds, 'deltas': deltas, 'zero_points': zero_points}
    _L0_cond_all = _L0_cond_setup()
    _L0_cond_in = {k: v for k, v in _L0_cond_all.items() if k in ()}
    del _L0_cond_all

    def _L1_cond_setup():
        import jax, jax.numpy as jnp
        import numpy as np
        MAX_LORAS, OUT, IN = (8, 1024, 1024)
        B, S = (4, 512)
        key = jax.random.key(seed)
        k1, k2, k3 = jax.random.split(key, 3)
        x = jax.random.normal(k1, (B, S, IN), dtype=jnp.float32)
        weight = jax.random.normal(k2, (MAX_LORAS, OUT, IN), dtype=jnp.float32) * 0.02
        adapter_ids = jax.random.randint(k3, (B,), 0, MAX_LORAS, dtype=jnp.int32)
        return {'x': x, 'weight': weight, 'adapter_ids': adapter_ids}
    _L1_cond_all = _L1_cond_setup()
    _L1_cond_in = {k: v for k, v in _L1_cond_all.items() if k in ('weight',)}
    del _L1_cond_all

    def _L2_cond_setup():
        import jax, jax.numpy as jnp
        import numpy as np
        B, S, D_IN, D_OUT = (4, 512, 1024, 1024)
        R, NUM_LABELERS = (32, 5)
        LORA_SCALING = 16 / 32
        key = jax.random.key(seed)
        k1, k2, k3, k4, k5 = jax.random.split(key, 5)
        x = jax.random.normal(k1, (B, S, D_IN), dtype=jnp.float32)
        labeler_index = jax.random.randint(k2, (B,), 0, NUM_LABELERS, dtype=jnp.int64)
        W = jax.random.normal(k3, (D_OUT, D_IN), dtype=jnp.float32) * 0.02
        lora_A = jax.random.normal(k4, (NUM_LABELERS, D_IN, R), dtype=jnp.float32) * 0.02
        lora_B_w = jax.random.normal(k5, (D_OUT, R), dtype=jnp.float32) * 0.02
        return {'x': x, 'labeler_index': labeler_index, 'W': W, 'lora_A': lora_A, 'lora_B_w': lora_B_w}
    _L2_cond_all = _L2_cond_setup()
    _L2_cond_in = {k: v for k, v in _L2_cond_all.items() if k in ('W', 'lora_A', 'lora_B_w')}
    del _L2_cond_all

    def _L3_cond_setup():
        import jax, jax.numpy as jnp
        import numpy as np
        RANK = 16
        ALPHA = 16.0
        SCALING = ALPHA / RANK
        N_ADAPTERS = 8
        IN_F = 1024
        OUT_F = 1024
        BATCH = 4
        SEQ = 512
        key = jax.random.key(seed)
        kx, ka, kb, ki = jax.random.split(key, 4)
        x = jax.random.normal(kx, (BATCH, SEQ, IN_F), dtype=jnp.float32)
        A = jax.random.normal(ka, (N_ADAPTERS, OUT_F, RANK), dtype=jnp.float32) * 0.02
        B = jax.random.normal(kb, (N_ADAPTERS, RANK, IN_F), dtype=jnp.float32) * 0.02
        adapter_ids = jax.random.randint(ki, (BATCH,), 0, N_ADAPTERS, dtype=jnp.int32)
        return {'x': x, 'A': A, 'B': B, 'adapter_ids': adapter_ids}
    _L3_cond_all = _L3_cond_setup()
    _L3_cond_in = {k: v for k, v in _L3_cond_all.items() if k in ('A', 'B')}
    del _L3_cond_all
    return {'x': x, 'condB_thresholds': condB_thresholds, 'condB_deltas': condB_deltas, 'condB_zeropoints': condB_zeropoints, 'itok_B_3_7': itok_B_3_7, 'itok_B_0_2': itok_B_0_2, 'L1_cond_weight': _L1_cond_in['weight'], 'L2_cond_W': _L2_cond_in['W'], 'L2_cond_lora_A': _L2_cond_in['lora_A'], 'L2_cond_lora_B_w': _L2_cond_in['lora_B_w'], 'L3_cond_A': _L3_cond_in['A'], 'L3_cond_B': _L3_cond_in['B']}

def reference(x, condB_thresholds, condB_deltas, condB_zeropoints, itok_B_3_7, itok_B_0_2, L1_cond_weight, L2_cond_W, L2_cond_lora_A, L2_cond_lora_B_w, L3_cond_A, L3_cond_B):
    import jax
    import jax.numpy as jnp

    def _L0_cond_ref(x, thresholds, deltas, zero_points):
        import jax, jax.numpy as jnp
        import numpy as np
        N_LEVELS = 64
        G = thresholds.shape[0]
        gi = jnp.sum(jnp.abs(x)[..., None] <= thresholds, axis=-1)
        idx = jnp.minimum(gi, G - 1)
        d = deltas[idx]
        zp = zero_points[idx]
        x_quant = jnp.clip(jnp.round(x / d) + zp, 0, N_LEVELS - 1)
        x_dequant = (x_quant - zp) * d
        return jnp.where(gi == G, jnp.float32(0), x_dequant)

    def _L1_cond_ref(x, weight, adapter_ids):
        import jax, jax.numpy as jnp
        import numpy as np
        MAX_LORAS, OUT, IN = (8, 1024, 1024)
        B, S = (4, 512)
        w = weight[adapter_ids]
        return jnp.einsum('bsi,boi->bso', x, w)

    def _L2_cond_ref(x, labeler_index, W, lora_A, lora_B_w):
        import jax, jax.numpy as jnp
        import numpy as np
        B, S, D_IN, D_OUT = (4, 512, 1024, 1024)
        R, NUM_LABELERS = (32, 5)
        LORA_SCALING = 16 / 32
        base = jnp.einsum('bsi,oi->bso', x, W)
        labelers_A = lora_A[labeler_index]
        low = jnp.einsum('bsi,bir->bsr', x, labelers_A)
        delta = jnp.einsum('bsr,or->bso', low, lora_B_w) * LORA_SCALING
        return base + delta

    def _L3_cond_ref(x, A, B, adapter_ids):
        import jax, jax.numpy as jnp
        import numpy as np
        RANK = 16
        ALPHA = 16.0
        SCALING = ALPHA / RANK
        N_ADAPTERS = 8
        IN_F = 1024
        OUT_F = 1024
        BATCH = 4
        SEQ = 512
        B_sel = B[adapter_ids]
        A_sel = A[adapter_ids]
        Bx = jnp.einsum('bni,bri->bnr', x, B_sel)
        out = jnp.einsum('bnr,bor->bno', Bx, A_sel)
        return out * SCALING
    x = x + _L0_cond_ref(x, condB_thresholds, condB_deltas, condB_zeropoints)
    x = x + _L1_cond_ref(x, L1_cond_weight, itok_B_3_7)
    x = x + _L2_cond_ref(x, itok_B_0_2, L2_cond_W, L2_cond_lora_A, L2_cond_lora_B_w)
    x = x + _L3_cond_ref(x, L3_cond_A, L3_cond_B, itok_B_3_7)
    return x

_drawn_inputs = setup_inputs


def setup_inputs(seed=0):
    import zlib

    import numpy as np

    out = dict(_drawn_inputs(seed))
    spreads = {}
    factors = {}
    for name, (base, spread) in spreads.items():
        noise = np.random.default_rng([zlib.crc32(name.encode()), seed]).standard_normal(out[name].shape)
        drawn = base * np.exp(spread * noise) if base else spread * noise
        out[name] = jnp.asarray(drawn.astype(out[name].dtype))
    for name, factor in factors.items():
        out[name] = (out[name] * factor).astype(out[name].dtype)
    return out
```

```python
import concourse.bass as bass
from concourse import mybir
from contextlib import ExitStack


def quantised_residual_adapter_stack(nc, x, params, w1, w2t, w2n, b3t, b2n, b2r, a3, la, ids_b, ids_a,
                                     own_rows, low_scale, out, e_dram, g_dram):
    f32, f32r, bf16, i16 = mybir.dt.float32, mybir.dt.float32r, mybir.dt.bfloat16, mybir.dt.int16
    ALU = mybir.AluOpType
    ACT = mybir.ActivationFunctionType

    P = 128
    B, _, KT, T = x.shape
    OT = KT
    G = params.shape[2]
    NA = w1.shape[0]
    NL = la.shape[0]
    R2 = b2n.shape[2]
    R3 = a3.shape[0] // NA
    R = R2 + R3
    D = KT * P
    HALF = KT // 2
    CH = HALF * T
    TOP_LEVEL = 63.0
    MAGIC = 1.5 * 2.0 ** 23
    BANKS = 4
    TILES = 2 * OT
    STEPS = 2 * G
    MASKS = STEPS - 2
    DUP = 64
    EH = NA * R2 // P
    LAST = B - 1

    ctx = ExitStack()
    with ctx:
        def sb(name, shape, dt=f32):
            return ctx.enter_context(nc.sbuf_tensor(name, shape, dt))

        def pb(name):
            return ctx.enter_context(nc.psum_tensor(name, [P, 512], f32))

        def sem(name):
            return ctx.enter_context(nc.semaphore(name))

        xin = sb("xin", [P, KT, T])
        x1 = sb("x1", [P, KT, T])
        x2 = sb("x2", [P, KT, T])
        x2h = sb("x2h", [P, KT, T], f32r)
        x2l = sb("x2l", [P, KT, T], f32r)
        outb = sb("outb", [P, OT, T])
        w1b = sb("w1b", [P, OT, KT * P])
        w2h = sb("w2h", [P, OT, KT * P], f32r)
        w2l = sb("w2l", [P, OT, KT * P], f32r)
        stage = sb("stage", [P, 2, KT * P])
        absx = sb("absx", [P, CH])
        tq = sb("tq", [P, 2, CH])
        uq = sb("uq", [P, 2, CH])
        mask = sb("mask", [P, 2, CH], bf16)
        y = sb("y", [P, CH])
        par = sb("par", [P, 3, G])
        top = sb("top", [P, 8])
        negtop = sb("negtop", [P, 8])
        rdelta = sb("rdelta", [P, G])
        ylow = sb("ylow", [P, G])
        yhigh = sb("yhigh", [P, G])
        magic = sb("magic", [P, 1])
        lscale = sb("lscale", [P, 1])
        rows = sb("rows", [P, NA])
        dmask = sb("dmask", [P, NA, R2])
        ua = sb("ua", [P, D])
        uhh = sb("uhh", [P, D], f32r)
        ul0 = sb("ul0", [P, D], f32r)
        va = sb("va", [P, KT, R2])
        vg = sb("vg", [P, KT, R3])
        vh = sb("vh", [P, KT, P], f32r)
        vl = sb("vl", [P, KT, P], f32r)
        lowh = sb("lowh", [P, T], f32r)
        lows = sb("lows", [P, T], f32r)
        b3s = w1b[:, OT - 1, :].rearrange("p (k r) -> p k r", k=KT)
        b2s = w1b[:, OT - 2, 0:KT * R2].rearrange("p (k r) -> p k r", k=KT)
        ycut = uq[:, 1, :]
        gsb = ua[:, :].rearrange("p (a k r) -> p a k r", a=NA, k=KT)
        a3s = outb[:, 0:HALF, :].rearrange("p k t -> p (k t)")
        b2rep = outb[:, HALF:KT, :].rearrange("p k t -> p (k t)")
        esb = x2[:, :, :].rearrange("p (h k) t -> p h (k t)", h=EH)

        bank = [pb(f"bank{i}") for i in range(BANKS)]
        low_bank = pb("low_bank")
        g_bank = [pb(f"g_bank{i}") for i in range(2)]
        e_bank = pb("e_bank")

        par_in = sem("par_in")
        x_in = [sem(f"x_in{c}") for c in range(2)]
        w1_in = [sem(f"w1_in{j}") for j in range(OT // 2)]
        small_in = sem("small_in")
        stage_in = [sem(f"stage_in{c}") for c in range(2)]
        u_in = sem("u_in")
        v_in = sem("v_in")
        store_done = [sem(f"store_done{c}") for c in range(2)]
        pads = sem("pads")
        par_step = sem("par_step")
        abs_ready = sem("abs_ready")
        t_ready = sem("t_ready")
        mask_ready = sem("mask_ready")
        u_ready = sem("u_ready")
        clamped = sem("clamped")
        y_ready = sem("y_ready")
        y_cut = sem("y_cut")
        x1_ready = sem("x1_ready")
        tile_done = sem("tile_done")
        banks_free = sem("banks_free")
        x2h_ready = sem("x2h_ready")
        x2l_ready = sem("x2l_ready")
        vh_ready = sem("vh_ready")
        vl_ready = sem("vl_ready")
        uh_ready = sem("uh_ready")
        ul_ready = sem("ul_ready")
        low_done = sem("low_done")
        lowh_ready = sem("lowh_ready")
        lows_ready = sem("lows_ready")
        d_done = sem("d_done")
        dmask_ready = sem("dmask_ready")
        g_done = sem("g_done")
        g_ready = sem("g_ready")
        e_done = sem("e_done")
        e_ready = sem("e_ready")
        w2h_ready = sem("w2h_ready")
        w2l_ready = sem("w2l_ready")

        block = ctx.enter_context(nc.Block())

        def chunk(t, c):
            return t[:, c * HALF:(c + 1) * HALF, :].rearrange("p k t -> p (k t)")

        def group_of(s):
            return G - 1 - s % G

        def tiles_read(n):
            return BANKS + n

        @block.sync
        def _(sp):
            def load_x(b, c):
                cut = slice(c * HALF, (c + 1) * HALF)
                sp.dma_start(xin[:, cut, :], x[bass.ds(b, 1), :, cut, :].rearrange("b p k t -> (b p) k t")) \
                    .then_inc(x_in[c], 16)

            def load_w1(a, j):
                sp.dma_start(w1b[:, 2 * j:2 * j + 2, :],
                             w1[bass.ds(a, 1), :, 2 * j:2 * j + 2, :].rearrange("a p j n -> (a p) j n")) \
                    .then_inc(w1_in[j], 16)

            def load_uv(a, lab):
                for r in (0, DUP):
                    sp.dma_start(ua[r:r + R2, :], e_dram[bass.ds(a, 1)].rearrange("a r n -> (a r) n")) \
                        .then_inc(u_in, 16)
                    sp.dma_start(ua[r + R2:r + R, :], a3[bass.ds(a * R3, R3), :]).then_inc(u_in, 16)
                sp.dma_start(va[:, :, :], la[bass.ds(lab, 1)].rearrange("a p k r -> (a p) k r")) \
                    .then_inc(v_in, 16)
                sp.dma_start(vg[:, :, :], g_dram[bass.ds(a, 1)].rearrange("a p k r -> (a p) k r")) \
                    .then_inc(v_in, 16)

            def ids_of(b):
                a = sp.value_load(ids_a[0:1, bass.ds(b, 1)], min_val=0, max_val=NA - 1)
                lab = sp.value_load(ids_b[0:1, bass.ds(b, 1)], min_val=0, max_val=NL - 1)
                return a, lab

            def store(b, c):
                cut = slice(c * HALF, (c + 1) * HALF)
                sp.dma_start(out[bass.ds(b, 1), :, cut, :].rearrange("b p k t -> (b p) k t"),
                             outb[:, cut, :]).then_inc(store_done[c], 16)

            sp.dma_start(par[:, :, :], params[:, :, :]).then_inc(par_in, 16)
            load_x(0, 0)
            load_x(0, 1)
            for dst, src in ((b3s, b3t), (b2s, b2n), (a3s, a3), (b2rep, b2r), (rows[:, :], own_rows),
                             (lscale[:, :], low_scale)):
                sp.dma_start(dst, src).then_inc(small_in, 16)
            a0, lab0 = ids_of(0)
            for i in range(KT):
                if i >= 2:
                    sp.wait_ge(g_done, i - 1)
                sp.dma_start(stage[:, i % 2, :], w2n[i, :, :]).then_inc(stage_in[i % 2], 16)
                if i % 2 == 1 and i // 2 < OT // 2 - 1:
                    load_w1(a0, i // 2)
            for i in range(OT):
                if i < 2:
                    sp.wait_ge(g_done, KT - 1 + i)
                else:
                    sp.wait_ge(w2l_ready, i - 1)
                sp.dma_start(stage[:, i % 2, :], w2t[i, :, :]).then_inc(stage_in[i % 2], 16)
                if i == 1:
                    sp.wait_ge(g_ready, KT)
                    load_w1(a0, OT // 2 - 1)
                    sp.dma_start(g_dram.rearrange("a p k r -> p a k r"), gsb[:, :, :, :]) \
                        .then_inc(store_done[0], 16)
                    sp.wait_ge(e_ready, 2 * EH)
                    sp.dma_start(e_dram.rearrange("(h a) r n -> (a r) h n", h=EH), esb) \
                        .then_inc(store_done[1], 16)
            sp.wait_ge(store_done[0], 16)
            sp.wait_ge(store_done[1], 16)
            sp.wait_ge(pads, 4)
            load_uv(a0, lab0)
            for c in range(2):
                sp.wait_ge(x1_ready, c + 1)
                load_x(1, c)

            def next_batch(b, ahead):
                a, lab = ids_of(b + 1)
                for j in range(OT // 2):
                    sp.wait_ge(tile_done, TILES * b + 2 * j + 2)
                    load_w1(a, j)
                if ahead:
                    sp.wait_ge(x1_ready, 2 * (b + 1) + 1)
                    load_x(b + 2, 0)
                sp.wait_ge(vl_ready, 4 * (b + 1))
                sp.wait_ge(ul_ready, b + 1)
                load_uv(a, lab)
                for c in range(2):
                    sp.wait_ge(banks_free, tiles_read(TILES * b + OT + (c + 1) * HALF))
                    store(b, c)
                if ahead:
                    sp.wait_ge(x1_ready, 2 * (b + 1) + 2)
                    load_x(b + 2, 1)

            with sp.Fori(0, LAST - 1) as b:
                next_batch(b, True)
            next_batch(LAST - 1, False)
            for c in range(2):
                sp.wait_ge(banks_free, tiles_read(TILES * LAST + OT + (c + 1) * HALF))
                store(LAST, c)
            for c in range(2):
                sp.wait_ge(store_done[c], 16 * (B + 1))

        @block.gpsimd
        def _(pool):
            for o in range(OT):
                pool.wait_ge(w2h_ready, o + 1)
                nc.gpsimd.tensor_tensor(w2l[:, o, :], stage[:, o % 2, :], w2h[:, o, :].bitcast(f32),
                                        ALU.subtract).then_inc(w2l_ready, 1)

        @block.scalar
        def _(act):
            def quantiser(b, s, first):
                c, g = s // G, group_of(s)
                n = STEPS * b + s
                if s % G == 0:
                    act.wait_ge(x_in[c], 16 * (b + 1))
                if not (first and s < 2):
                    act.wait_ge(u_ready, n - 1)
                nc.scalar.activation(tq[:, s % 2, :], chunk(xin, c), ACT.Identity, bias=magic[:, 0:1],
                                     scale=rdelta[:, g:g + 1]).then_inc(t_ready, 1)
                if s % G == 1:
                    if not (first and c == 0):
                        act.wait_ge(y_cut, 2 * b + c)
                    nc.scalar.activation(absx[:, :], chunk(xin, c), ACT.Abs).then_inc(abs_ready, 1)
                    act.wait_ge(abs_ready, 2 * b + c + 1)
                if s % G:
                    if not (first and s < 3):
                        act.wait_ge(y_ready, n - 1)
                    nc.scalar.activation(mask[:, s % 2, :], absx[:, :], ACT.Relu,
                                         bias=negtop[:, g:g + 1], scale=1.0).then_inc(mask_ready, 1)

            def round_x2(b, k):
                act.wait_ge(banks_free, tiles_read(TILES * b + k + 1))
                nc.scalar.activation(x2h[:, k, :], x2[:, k, :], ACT.Copy).then_inc(x2h_ready, 1)

            def round_v(b):
                act.wait_ge(v_in, 32 * (b + 1))
                act.wait_ge(banks_free, tiles_read(TILES * b))
                for at in (0, DUP):
                    nc.scalar.activation(vh[:, :, at:at + R2], va[:, :, :], ACT.Copy).then_inc(vh_ready, 1)
                    nc.scalar.activation(vh[:, :, at + R2:at + R], vg[:, :, :], ACT.Copy).then_inc(vh_ready, 1)

            def round_u(b):
                act.wait_ge(u_in, 64 * (b + 1))
                nc.scalar.activation(uhh[:, :], ua[:, :], ACT.Copy).then_inc(uh_ready, 1)

            def round_low(b):
                act.wait_ge(low_done, b + 1)
                nc.scalar.activation(lowh[:, :], low_bank[:, 0:T], ACT.Copy, scale=lscale[:, 0:1]) \
                    .then_inc(lowh_ready, 1)
                nc.scalar.activation(lows[0:DUP, :], low_bank[0:DUP, 0:T], ACT.Copy,
                                     scale=lscale[0:DUP, 0:1]).then_inc(lowh_ready, 1)

            act.wait_ge(par_step, 7)
            act.wait_ge(pads, 3)
            for s in range(STEPS):
                quantiser(0, s, True)
            act.wait_ge(small_in, 96)
            for o in range(OT):
                act.wait_ge(stage_in[o % 2], 16 * (KT // 2 + o // 2 + 1))
                nc.scalar.activation(w2h[:, o, :], stage[:, o % 2, :], ACT.Copy).then_inc(w2h_ready, 1)

            def batch(b, quantise):
                for s in range(STEPS):
                    if s == 2:
                        round_v(b)
                    if s == 4:
                        round_u(b)
                    if 1 <= s <= KT:
                        round_x2(b, s - 1)
                    if s == KT + 1:
                        round_low(b)
                    if quantise:
                        quantiser(b + 1, s, False)

            with act.Fori(0, LAST) as b:
                batch(b, True)
            batch(LAST, False)

        @block.vector
        def _(dve):
            def await_value(b, s):
                if s % G:
                    dve.wait_ge(y_ready, STEPS * b + s)
                    n = MASKS * b + s - s // G
                    dve.wait_ge(clamped, n)
                    dve.wait_ge(mask_ready, n)

            def select(s):
                if s % G:
                    nc.vector.copy_predicated(y[:, :], mask[:, s % 2, :].bitcast(i16), uq[:, s % 2, :]) \
                        .then_inc(y_ready, 1)

            def quantiser(b, s):
                g = group_of(s)
                n = STEPS * b + s
                dve.wait_ge(t_ready, n + 1)
                if s % G < 2:
                    dve.wait_ge(x1_ready, 2 * b + (s - 1) // G if s else 2 * b)
                if s:
                    await_value(b, s - 1)
                nc.vector.tensor_scalar(uq[:, s % 2, :], tq[:, s % 2, :], -MAGIC, par[:, 1, g:g + 1],
                                        ALU.add, ALU.mult).then_inc(u_ready, 1)
                if s:
                    select(s - 1)
                if s == G:
                    cut_y(b, 0)
                    dve.wait_ge(y_cut, 2 * b + 1)
                dve.wait_ge(u_ready, n + 1)
                clamped_y = uq[:, s % 2, :] if s % G else y[:, :]
                nc.vector.tensor_scalar(clamped_y, uq[:, s % 2, :], ylow[:, g:g + 1], yhigh[:, g:g + 1],
                                        ALU.max, ALU.min).then_inc(clamped if s % G else y_ready, 1)

            def cut_y(b, c):
                dve.wait_ge(y_ready, STEPS * b + G * (c + 1))
                nc.vector.scalar_tensor_tensor(ycut, absx[:, :], top[:, G - 1:G], y[:, :],
                                               ALU.is_gt, ALU.mult).then_inc(y_cut, 1)

            def add_y(b, c):
                dve.wait_ge(y_cut, 2 * b + c + 1)
                nc.vector.tensor_tensor(chunk(x1, c), chunk(xin, c), ycut, ALU.add) \
                    .then_inc(x1_ready, 1)

            def finish_x2(b, k):
                dve.wait_ge(tile_done, TILES * b + k + 1)
                nc.vector.tensor_tensor(x2[:, k, :], bank[k % BANKS][:, 0:T], x1[:, k, :], ALU.add) \
                    .then_inc(banks_free, 1)

            def split_x2(b, k):
                dve.wait_ge(x2h_ready, KT * b + k + 1)
                nc.vector.tensor_tensor(x2l[:, k, :], x2[:, k, :], x2h[:, k, :].bitcast(f32), ALU.subtract) \
                    .then_inc(x2l_ready, 1)

            def finish_out(b, o):
                if o % HALF == 0:
                    dve.wait_ge(store_done[o // HALF], 16 * (b + 1))
                dve.wait_ge(tile_done, TILES * b + OT + o + 1)
                nc.vector.tensor_tensor(outb[:, o, :], bank[o % BANKS][:, 0:T], x2[:, o, :], ALU.add) \
                    .then_inc(banks_free, 1)

            def split_v(b):
                dve.wait_ge(vh_ready, 4 * (b + 1))
                for at in (0, DUP):
                    for src, lo, hi in ((va, at, at + R2), (vg, at + R2, at + R)):
                        nc.vector.tensor_tensor(vl[:, :, lo:hi], src[:, :, :], vh[:, :, lo:hi].bitcast(f32),
                                                ALU.subtract).then_inc(vl_ready, 1)

            def split_u(b):
                dve.wait_ge(uh_ready, b + 1)
                nc.vector.tensor_tensor(ul0[0:DUP, :], ua[0:DUP, :], uhh[0:DUP, :].bitcast(f32),
                                        ALU.subtract).then_inc(ul_ready, 1)

            def split_low(b):
                dve.wait_ge(lowh_ready, 2 * (b + 1))
                nc.vector.scalar_tensor_tensor(lows[DUP:P, :], low_bank[DUP:P, 0:T], lscale[DUP:P, 0:1],
                                               lowh[DUP:P, :].bitcast(f32), ALU.mult, ALU.subtract) \
                    .then_inc(lows_ready, 1)

            nc.vector.memset(magic[:, :], MAGIC).then_inc(pads, 1)
            nc.vector.memset(vh[:, :, :].bitcast(f32), 0.0).then_inc(pads, 1)
            nc.vector.memset(vl[:, :, :].bitcast(f32), 0.0).then_inc(pads, 1)
            nc.vector.memset(ul0[:, :].bitcast(f32), 0.0).then_inc(banks_free, BANKS)
            dve.wait_ge(par_in, 16)
            nc.vector.max(top[:, :], par[:, 0, :]).then_inc(par_step, 1)
            nc.vector.reciprocal(rdelta[:, :], par[:, 1, :]).then_inc(par_step, 1)
            nc.vector.tensor_scalar(ylow[:, :], par[:, 2, :], -1.0, None, ALU.mult).then_inc(par_step, 1)
            nc.vector.tensor_scalar(yhigh[:, :], par[:, 2, :], -1.0, TOP_LEVEL, ALU.mult, ALU.add) \
                .then_inc(par_step, 1)
            dve.wait_ge(par_step, 4)
            nc.vector.tensor_scalar(negtop[:, :], top[:, :], -1.0, None, ALU.mult).then_inc(par_step, 1)
            nc.vector.tensor_tensor(ylow[:, :], ylow[:, :], par[:, 1, :], ALU.mult).then_inc(par_step, 1)
            nc.vector.tensor_tensor(yhigh[:, :], yhigh[:, :], par[:, 1, :], ALU.mult).then_inc(par_step, 1)
            dve.wait_ge(par_step, 7)

            def adapters_part(s):
                if s == 1:
                    dve.wait_ge(d_done, 1)
                    for a in range(NA):
                        nc.vector.tensor_scalar(dmask[:, a, :], e_bank[:, 0:R2], rows[:, a:a + 1], None,
                                                ALU.mult).then_inc(dmask_ready, 1)
                if 2 <= s < 2 + KT:
                    i = s - 2
                    dve.wait_ge(g_done, i + 1)
                    nc.vector.tensor_tensor(gsb[:, :, i, :],
                                            g_bank[i % 2][:, 0:NA * R3].rearrange("p (a r) -> p a r", a=NA),
                                            b3s[:, i, :].rearrange("p (a r) -> p a r", a=NA), ALU.add) \
                        .then_inc(g_ready, 1)
                if 2 + KT <= s < 2 + KT + 2 * EH:
                    h, n = divmod(s - 2 - KT, 2)
                    cut = slice(n * 512, (n + 1) * 512)
                    dve.wait_ge(e_done, 2 * h + n + 1)
                    nc.vector.tensor_tensor(esb[:, h, cut], e_bank[:, :], b2rep[:, cut], ALU.add) \
                        .then_inc(e_ready, 1)

            for s in range(STEPS):
                quantiser(0, s)
                adapters_part(s)
                if s == G:
                    add_y(0, 0)
            await_value(0, STEPS - 1)
            select(STEPS - 1)
            cut_y(0, 1)
            add_y(0, 1)
            for c in range(2):
                dve.wait_ge(store_done[c], 16)
            nc.vector.memset(ua[:, :], 0.0).then_inc(pads, 1)

            def batch(b, quantise):
                for s in range(STEPS):
                    if 1 <= s <= KT:
                        finish_x2(b, s - 1)
                    if s == KT:
                        split_x2(b, KT - 1)
                    if s == 3:
                        split_v(b)
                    if s == 5:
                        split_u(b)
                    if s == KT + 1:
                        split_low(b)
                    if KT < s < STEPS - 1:
                        finish_out(b, s - KT - 1)
                    if quantise:
                        quantiser(b + 1, s)
                    if quantise and s == KT:
                        add_y(b + 1, 0)
                    if 1 <= s < KT:
                        split_x2(b, s - 1)
                if quantise:
                    await_value(b + 1, STEPS - 1)
                finish_out(b, OT - 2)
                if quantise:
                    select(STEPS - 1)
                    cut_y(b + 1, 1)
                    add_y(b + 1, 1)
                finish_out(b, OT - 1)

            with dve.Fori(0, LAST) as b:
                batch(b, True)
            batch(LAST, False)

        @block.tensor
        def _(pe):
            pe.wait_ge(small_in, 96)
            for k in range(KT):
                last = nc.tensor.matmul(e_bank[:, 0:R2], b3s[:, k, :], b2s[:, k, :],
                                        start=(k == 0), stop=(k == KT - 1))
            last.then_inc(d_done, 1)
            for i in range(KT):
                pe.wait_ge(stage_in[i % 2], 16 * (i // 2 + 1))
                if i >= 2:
                    pe.wait_ge(g_ready, i - 1)
                for o in range(OT):
                    last = nc.tensor.matmul(g_bank[i % 2][:, 0:NA * R3], stage[:, i % 2, o * P:(o + 1) * P],
                                            b3s[:, o, :], start=(o == 0), stop=(o == OT - 1))
                last.then_inc(g_done, 1)
            pe.wait_ge(dmask_ready, NA)
            for h in range(EH):
                for n in range(2):
                    if 2 * h + n:
                        pe.wait_ge(e_ready, 2 * h + n)
                    per = P // R2
                    nc.tensor.matmul(e_bank[:, :], dmask[:, h * per:(h + 1) * per, :].rearrange("p a r -> p (a r)"),
                                     a3s[:, n * 512:(n + 1) * 512], start=True, stop=True).then_inc(e_done, 1)

            def free_bank(b, s):
                pe.wait_ge(banks_free, TILES * b + s + 1)
                return bank[s % BANKS][:, 0:T]

            def batch(b):
                for o in range(OT):
                    if o % 2 == 0:
                        pe.wait_ge(w1_in[o // 2], 16 * (b + 1))
                    into = free_bank(b, o)
                    for k in range(KT):
                        if o == 0 and k % HALF == 0:
                            pe.wait_ge(x1_ready, 2 * b + k // HALF + 1)
                        last = nc.tensor.matmul(into, w1b[:, o, k * P:(k + 1) * P], x1[:, k, :],
                                                start=(k == 0), stop=(k == KT - 1))
                    last.then_inc(tile_done, 1)
                pe.wait_ge(vl_ready, 4 * (b + 1))
                for k in range(KT):
                    pe.wait_ge(x2l_ready, KT * b + k + 1)
                    for i, (v, xs) in enumerate(((vh, x2h), (vl, x2h), (vh, x2l))):
                        last = nc.tensor.matmul(low_bank[:, 0:T], v[:, k, :], xs[:, k, :],
                                                start=(k == 0 and i == 0), stop=(k == KT - 1 and i == 2))
                last.then_inc(low_done, 1)
                for o in range(OT):
                    into = free_bank(b, OT + o)
                    if o % 2 == 0:
                        pe.wait_ge(w2l_ready, o + 2)
                    for k in range(KT):
                        cut = slice(k * P, (k + 1) * P)
                        for i, (w, xs) in enumerate(((w2h, x2h), (w2l, x2h), (w2h, x2l))):
                            nc.tensor.matmul(into, w[:, o, cut], xs[:, k, :], start=(k == 0 and i == 0),
                                             stop=False)
                    if o == 0:
                        pe.wait_ge(lows_ready, b + 1)
                        pe.wait_ge(ul_ready, b + 1)
                    cut = slice(o * P, (o + 1) * P)
                    nc.tensor.matmul(into, uhh[:, cut], lows[:, :], start=False, stop=False)
                    nc.tensor.matmul(into, ul0[:, cut], lows[:, :], start=False, stop=True).then_inc(tile_done, 1)

            with pe.Fori(0, B) as b:
                batch(b)


def kernel(**inputs):
    import numpy as np
    import concourse.bacc as bacc
    from concourse.bass_utils import run_bass_kernel_spmd

    P = 128
    x = np.asarray(inputs["x"])
    B, T, D = x.shape
    KT = D // P
    w1 = np.asarray(inputs["L1_cond_weight"])
    w2 = np.asarray(inputs["L2_cond_W"])
    la = np.asarray(inputs["L2_cond_lora_A"])
    b2 = np.asarray(inputs["L2_cond_lora_B_w"])
    a3 = np.asarray(inputs["L3_cond_A"])
    b3 = np.asarray(inputs["L3_cond_B"])
    NA, NL, R2, R3 = w1.shape[0], la.shape[0], la.shape[2], a3.shape[2]
    params = np.stack([np.asarray(inputs[n]) for n in
                       ("condB_thresholds", "condB_deltas", "condB_zeropoints")])
    row = np.arange(P)
    arrays = {
        "x": x.reshape(B, T, KT, P).transpose(0, 3, 2, 1),
        "params": np.broadcast_to(params, (P,) + params.shape),
        "w1": w1.reshape(NA, KT, P, KT, P).transpose(0, 4, 1, 3, 2).reshape(NA, P, KT, D),
        "w2t": w2.reshape(KT, P, KT, P).transpose(0, 3, 2, 1).reshape(KT, P, D),
        "w2n": w2.reshape(KT, P, KT, P).transpose(2, 1, 0, 3).reshape(KT, P, D),
        "b3t": b3.reshape(NA * R3, KT, P).transpose(2, 1, 0),
        "b2n": b2.reshape(KT, P, R2).transpose(1, 0, 2),
        "b2r": np.tile(b2.T, (P // R2, 1)),
        "a3": a3.transpose(0, 2, 1).reshape(NA * R3, D),
        "la": la.reshape(NL, KT, P, R2).transpose(0, 2, 1, 3),
        "ids_b": np.asarray(inputs["itok_B_0_2"]).reshape(1, B),
        "ids_a": np.asarray(inputs["itok_B_3_7"]).reshape(1, B),
        "own_rows": (row[:, None] // R3 == np.arange(NA)).astype(np.float32),
        "low_scale": np.where(row % 64 < R2, 0.5, 1.0).astype(np.float32)[:, None],
    }
    arrays = {n: np.ascontiguousarray(a) for n, a in arrays.items()}
    nc = bacc.Bacc("TRN2", target_bir_lowering=False, num_devices=1)
    args = {n: nc.dram_tensor(n, a.shape, mybir.dt.from_np(a.dtype), kind="ExternalInput").ap()
            for n, a in arrays.items()}
    args["out"] = nc.dram_tensor("out", (B, P, KT, T), mybir.dt.float32, kind="ExternalOutput").ap()
    args["e_dram"] = nc.dram_tensor("e_dram", (NA, R2, D), mybir.dt.float32, kind="Internal").ap()
    args["g_dram"] = nc.dram_tensor("g_dram", (NA, P, KT, R3), mybir.dt.float32, kind="Internal").ap()
    quantised_residual_adapter_stack(nc, **args)
    r = run_bass_kernel_spmd(nc, [arrays], core_ids=[0])
    got = np.asarray(r.results[0]["out"])
    return np.ascontiguousarray(got.transpose(0, 3, 2, 1).reshape(B, T, D))
```

```python
import concourse.bass as bass
from concourse import mybir
from contextlib import ExitStack


def quantised_residual_adapter_stack(nc, x, params, w1, w2t, w2n, b3t, b2n, b2r, a3, la, ids_b, ids_a,
                                     own_rows, low_scale, ident, out, e_dram, g_dram):
    f32, f32r, bf16, i16 = mybir.dt.float32, mybir.dt.float32r, mybir.dt.bfloat16, mybir.dt.int16
    ALU = mybir.AluOpType
    ACT = mybir.ActivationFunctionType

    P = 128
    B, _, KT, T = x.shape
    OT = KT
    G = params.shape[2]
    NA = w1.shape[0]
    NL = la.shape[0]
    R2 = b2n.shape[2]
    R3 = a3.shape[0] // NA
    R = R2 + R3
    D = KT * P
    HALF = KT // 2
    CH = HALF * T
    TOP_LEVEL = 63.0
    MAGIC = 1.5 * 2.0 ** 23
    PAIRS = OT // 2
    OUT_BANKS = 2
    STEPS = 2 * G
    MASKS = STEPS - 2
    DUP = 64
    EH = NA * R2 // P
    LAST = B - 1
    TQ, MK = 2, 4

    ctx = ExitStack()
    with ctx:
        def sb(name, shape, dt=f32):
            return ctx.enter_context(nc.sbuf_tensor(name, shape, dt))

        def pb(name):
            return ctx.enter_context(nc.psum_tensor(name, [P, 512], f32))

        def sem(name):
            return ctx.enter_context(nc.semaphore(name))

        xin = sb("xin", [P, KT, T])
        x1 = sb("x1", [P, KT, T])
        x2 = sb("x2", [P, 2, 2 * T])
        x2h = sb("x2h", [P, KT, T], f32r)
        x2l = sb("x2l", [P, KT, T], f32r)
        outb = sb("outb", [P, PAIRS, 2 * T])
        w1b = sb("w1b", [P, OT, KT * P])
        w2h = sb("w2h", [P, OT, KT * P], f32r)
        w2l = sb("w2l", [P, OT, KT * P], f32r)
        stage = sb("stage", [P, 2, KT * P])
        absx = sb("absx", [P, CH])
        tq = sb("tq", [P, TQ, CH])
        uq = sb("uq", [P, 2, CH])
        mask = sb("mask", [P, MK, CH], bf16)
        y = sb("y", [P, CH])
        par = sb("par", [P, 3, G])
        top = sb("top", [P, 8])
        negtop = sb("negtop", [P, 8])
        rdelta = sb("rdelta", [P, G])
        ylow = sb("ylow", [P, G])
        yhigh = sb("yhigh", [P, G])
        magic = sb("magic", [P, 1])
        top_spare = sb("top_spare", [P, 2])
        lscale = sb("lscale", [P, 1])
        rows = sb("rows", [P, NA])
        eye = sb("eye", [P, P])
        dmask = sb("dmask", [P, NA, R2])
        ua = sb("ua", [P, D])
        uhh = sb("uhh", [P, D], f32r)
        ul0 = sb("ul0", [P, D], f32r)
        va = sb("va", [P, KT, R2])
        vg = sb("vg", [P, KT, R3])
        vh = sb("vh", [P, KT, P], f32r)
        vl = sb("vl", [P, KT, P], f32r)
        lowh = sb("lowh", [P, T], f32r)
        lows = sb("lows", [P, T], f32r)
        b3s = w1b[:, OT - 1, :].rearrange("p (k r) -> p k r", k=KT)
        b2s = w1b[:, OT - 2, 0:KT * R2].rearrange("p (k r) -> p k r", k=KT)
        ycut = uq[:, 1, :]
        gsb = ua[:, :].rearrange("p (a k r) -> p a k r", a=NA, k=KT)
        a3s = outb[:, 0:2, :].rearrange("p j t -> p (j t)")
        b2rep = outb[:, 2:4, :].rearrange("p j t -> p (j t)")
        esb = x2

        x2_bank = [pb(f"x2_bank{i}") for i in range(PAIRS)]
        out_bank = [pb(f"out_bank{i}") for i in range(OUT_BANKS)]
        low_bank = pb("low_bank")
        de_bank = pb("de_bank")

        par_in = sem("par_in")
        x_in = [sem(f"x_in{c}") for c in range(2)]
        w1_in = [sem(f"w1_in{j}") for j in range(OT // 2)]
        small_in = sem("small_in")
        stage_in = [sem(f"stage_in{c}") for c in range(2)]
        u_in = sem("u_in")
        v_in = sem("v_in")
        store_done = [sem(f"store_done{c}") for c in range(2)]
        pads = sem("pads")
        ua_zero = sem("ua_zero")
        par_step = sem("par_step")
        abs_ready = sem("abs_ready")
        t_ready = sem("t_ready")
        mask_ready = sem("mask_ready")
        u_ready = sem("u_ready")
        clamped = sem("clamped")
        y_ready = sem("y_ready")
        y_cut = sem("y_cut")
        x1_ready = sem("x1_ready")
        pair_done = sem("pair_done")
        x2_ready = sem("x2_ready")
        out_ready = sem("out_ready")
        e_out = [sem(f"e_out{i}") for i in range(2)]
        eye_in = sem("eye_in")
        diag_ready = sem("diag_ready")
        x2h_ready = sem("x2h_ready")
        x2l_ready = sem("x2l_ready")
        vh_ready = sem("vh_ready")
        vl_ready = sem("vl_ready")
        uh_ready = sem("uh_ready")
        ul_ready = sem("ul_ready")
        low_done = sem("low_done")
        lowh_ready = sem("lowh_ready")
        lows_ready = sem("lows_ready")
        d_done = sem("d_done")
        dmask_ready = sem("dmask_ready")
        g_done = sem("g_done")
        g_ready = sem("g_ready")
        e_done = sem("e_done")
        e_ready = sem("e_ready")
        w2h_ready = sem("w2h_ready")
        w2l_ready = sem("w2l_ready")

        block = ctx.enter_context(nc.Block())

        def chunk(t, c):
            return t[:, c * HALF:(c + 1) * HALF, :].rearrange("p k t -> p (k t)")

        def group_of(s):
            return G - 1 - s % G

        def x2_pairs(n):
            return PAIRS + n

        def out_pairs(n):
            return OUT_BANKS + n

        @block.sync
        def _(sp):
            def load_x(b, c):
                cut = slice(c * HALF, (c + 1) * HALF)
                sp.dma_start(xin[:, cut, :], x[bass.ds(b, 1), :, cut, :].rearrange("b p k t -> (b p) k t")) \
                    .then_inc(x_in[c], 16)

            def load_w1(a, j):
                sp.dma_start(w1b[:, 2 * j:2 * j + 2, :],
                             w1[bass.ds(a, 1), :, 2 * j:2 * j + 2, :].rearrange("a p j n -> (a p) j n")) \
                    .then_inc(w1_in[j], 16)

            def load_uv(a, lab):
                for r in (0, DUP):
                    sp.dma_start(ua[r:r + R2, :], e_dram[bass.ds(a, 1)].rearrange("a r n -> (a r) n")) \
                        .then_inc(u_in, 16)
                    sp.dma_start(ua[r + R2:r + R, :], a3[bass.ds(a * R3, R3), :]).then_inc(u_in, 16)
                sp.dma_start(va[:, :, :], la[bass.ds(lab, 1)].rearrange("a p k r -> (a p) k r")) \
                    .then_inc(v_in, 16)
                sp.dma_start(vg[:, :, :], g_dram[bass.ds(a, 1)].rearrange("a p k r -> (a p) k r")) \
                    .then_inc(v_in, 16)

            def ids_of(b):
                a = sp.value_load(ids_a[0:1, bass.ds(b, 1)], min_val=0, max_val=NA - 1)
                lab = sp.value_load(ids_b[0:1, bass.ds(b, 1)], min_val=0, max_val=NL - 1)
                return a, lab

            def store(b, c):
                sp.dma_start(out[bass.ds(b, 1), :, 2 * c:2 * c + 2, :].rearrange("b p j t -> (b p) j t"),
                             outb[:, 2 * c:2 * c + 2, :]).then_inc(store_done[c], 16)

            sp.dma_start(par[:, :, :], params[:, :, :]).then_inc(par_in, 16)
            load_x(0, 0)
            for dst, src in ((b3s, b3t), (b2s, b2n), (rows[:, :], own_rows), (lscale[:, :], low_scale),
                             (a3s, a3), (b2rep, b2r)):
                sp.dma_start(dst, src).then_inc(small_in, 16)
            load_x(0, 1)
            sp.dma_start(eye[:, :], ident[:, :]).then_inc(eye_in, 16)
            a0, lab0 = ids_of(0)

            def store_e(e, done):
                h, n = divmod(e, 2)
                sp.wait_ge(e_ready, e + 1)
                sp.dma_start(e_dram.rearrange("(h a) r n -> h (a r) n", h=EH)[h, :, n * 512:(n + 1) * 512],
                             esb[:, e % 2, :]).then_inc(done, 16)

            for i in range(KT):
                if i >= 2:
                    sp.wait_ge(g_done, i - 1)
                sp.dma_start(stage[:, i % 2, :], w2n[i, :, :]).then_inc(stage_in[i % 2], 16)
                if i % 2 == 1 and i // 2 < PAIRS - 1:
                    load_w1(a0, i // 2)
                e = i - (KT - 2 * EH + 1)
                if e >= 0:
                    store_e(e, e_out[e % 2])
            for i in range(OT):
                if i < 2:
                    sp.wait_ge(g_done, KT - 1 + i)
                else:
                    sp.wait_ge(w2l_ready, i - 1)
                sp.dma_start(stage[:, i % 2, :], w2t[i, :, :]).then_inc(stage_in[i % 2], 16)
                if i == 1:
                    sp.wait_ge(x1_ready, 1)
                    load_x(1, 0)
                    sp.wait_ge(g_ready, 2)
                    sp.dma_start(g_dram.rearrange("a p k r -> p a k r"), gsb[:, :, :, :]) \
                        .then_inc(store_done[0], 16)
                    load_w1(a0, PAIRS - 1)
                    store_e(2 * EH - 1, store_done[1])
                    sp.wait_ge(store_done[0], 16)
                    sp.wait_ge(store_done[1], 16)
                    sp.wait_ge(e_out[0], 32)
                    sp.wait_ge(e_out[1], 16)
                    sp.wait_ge(ua_zero, 1)
                    load_uv(a0, lab0)
            sp.wait_ge(x1_ready, 2)
            load_x(1, 1)

            def next_batch(b, ahead):
                a, lab = ids_of(b + 1)
                for j in range(PAIRS):
                    sp.wait_ge(pair_done, 2 * PAIRS * b + j + 1)
                    load_w1(a, j)
                if ahead:
                    sp.wait_ge(x1_ready, 2 * (b + 1) + 1)
                    load_x(b + 2, 0)
                sp.wait_ge(vl_ready, 4 * (b + 1))
                sp.wait_ge(ul_ready, b + 1)
                load_uv(a, lab)
                for c in range(2):
                    sp.wait_ge(out_ready, out_pairs(PAIRS * b + 2 * c + 2))
                    store(b, c)
                if ahead:
                    sp.wait_ge(x1_ready, 2 * (b + 1) + 2)
                    load_x(b + 2, 1)

            with sp.Fori(0, LAST - 1) as b:
                next_batch(b, True)
            next_batch(LAST - 1, False)
            for c in range(2):
                sp.wait_ge(out_ready, out_pairs(PAIRS * LAST + 2 * c + 2))
                store(LAST, c)
            for c in range(2):
                sp.wait_ge(store_done[c], 16 * (B + 1))

        @block.gpsimd
        def _(pool):
            nc.gpsimd.memset(vh[:, :, :].bitcast(f32), 0.0).then_inc(pads, 1)
            nc.gpsimd.memset(vl[:, :, :].bitcast(f32), 0.0).then_inc(pads, 1)
            nc.gpsimd.memset(ul0[:, :].bitcast(f32), 0.0).then_inc(pads, 1)
            pool.wait_ge(eye_in, 16)
            for o in range(OT):
                pool.wait_ge(stage_in[o % 2], 16 * (KT // 2 + o // 2 + 1))
                diag = stage[:, o % 2, o * P:(o + 1) * P]
                nc.gpsimd.tensor_tensor(diag, diag, eye[:, :], ALU.add).then_inc(diag_ready, 1)
                pool.wait_ge(w2h_ready, o + 1)
                nc.gpsimd.tensor_tensor(w2l[:, o, :], stage[:, o % 2, :], w2h[:, o, :].bitcast(f32),
                                        ALU.subtract).then_inc(w2l_ready, 1)
                if o == 0:
                    pool.wait_ge(store_done[0], 16)
                    nc.gpsimd.memset(ua[:, :], 0.0).then_inc(ua_zero, 1)

        EARLY = 3

        def at(early, *steps):
            return [step - (EARLY if early else 0) for step in steps]

        @block.scalar
        def _(act):
            def quantiser(b, s, first=False):
                c, g = s // G, group_of(s)
                n = STEPS * b + s
                if s % G == 0:
                    act.wait_ge(x_in[c], 16 * (b + 1))
                if not (first and s < TQ):
                    act.wait_ge(u_ready, n - TQ + 1)
                nc.scalar.activation(tq[:, s % TQ, :], chunk(xin, c), ACT.Identity, bias=magic[:, 0:1],
                                     scale=rdelta[:, g:g + 1]).then_inc(t_ready, 1)
                if s % G == 1:
                    if not (first and c == 0):
                        act.wait_ge(y_cut, 2 * b + c)
                    nc.scalar.activation(absx[:, :], chunk(xin, c), ACT.Abs).then_inc(abs_ready, 1)
                    act.wait_ge(abs_ready, 2 * b + c + 1)
                if s % G:
                    if not (first and s < MK):
                        act.wait_ge(y_ready, n - MK + 1)
                    nc.scalar.activation(mask[:, s % MK, :], absx[:, :], ACT.Relu,
                                         bias=negtop[:, g:g + 1], scale=1.0).then_inc(mask_ready, 1)

            def round_x2(b, j):
                act.wait_ge(x2_ready, x2_pairs(PAIRS * b + j + 1))
                nc.scalar.activation(x2h[:, 2 * j:2 * j + 2, :].rearrange("p k t -> p (k t)"),
                                     x2[:, j % 2, :], ACT.Copy).then_inc(x2h_ready, 1)

            def round_v(b, first):
                act.wait_ge(v_in, 32 * (b + 1))
                if not first:
                    act.wait_ge(low_done, b)
                for c in (0, DUP):
                    nc.scalar.activation(vh[:, :, c:c + R2], va[:, :, :], ACT.Copy).then_inc(vh_ready, 1)
                    nc.scalar.activation(vh[:, :, c + R2:c + R], vg[:, :, :], ACT.Copy).then_inc(vh_ready, 1)

            def round_u(b, first):
                act.wait_ge(u_in, 64 * (b + 1))
                if not first:
                    act.wait_ge(pair_done, 2 * PAIRS * b)
                nc.scalar.activation(uhh[:, :], ua[:, :], ACT.Copy).then_inc(uh_ready, 1)

            def round_low(b):
                act.wait_ge(low_done, b + 1)
                nc.scalar.activation(lowh[:, :], low_bank[:, 0:T], ACT.Copy, scale=lscale[:, 0:1]) \
                    .then_inc(lowh_ready, 1)
                nc.scalar.activation(lows[0:DUP, :], low_bank[0:DUP, 0:T], ACT.Copy,
                                     scale=lscale[0:DUP, 0:1]).then_inc(lowh_ready, 1)

            def finish_out(b, j):
                if j % 2 == 0:
                    act.wait_ge(store_done[j // 2], 16 * (b + 1))
                act.wait_ge(pair_done, 2 * PAIRS * b + PAIRS + j + 1)
                nc.scalar.activation(outb[:, j, :], out_bank[j % OUT_BANKS][:, :], ACT.Copy) \
                    .then_inc(out_ready, 1)

            def round_w2(o):
                act.wait_ge(diag_ready, o + 1)
                nc.scalar.activation(w2h[:, o, :], stage[:, o % 2, :], ACT.Copy).then_inc(w2h_ready, 1)

            act.wait_ge(par_step, 7)
            for s in range(STEPS):
                quantiser(0, s, True)
            act.wait_ge(small_in, 96)
            act.wait_ge(pads, 4)
            round_w2(0)
            quantiser(1, 0)
            round_w2(1)
            quantiser(1, 1)

            def batch(b, steps, early=False):
                v_at, u_at, low_at = at(early, 5, 6, 10)
                x2_at = at(early, 6, 7, 8, 8)
                out_at = at(early, 12, 14, 15, 17)
                for s in range(2, STEPS + 2):
                    if s < 2 + steps:
                        quantiser(b + 1 + s // STEPS, s % STEPS)
                    if early and s < OT:
                        round_w2(s)
                    if s == v_at:
                        round_v(b, early)
                    if s == u_at:
                        round_u(b, early)
                    for j in range(PAIRS):
                        if s == x2_at[j]:
                            round_x2(b, j)
                    if s == low_at:
                        round_low(b)
                    for j in range(PAIRS):
                        if s == out_at[j]:
                            finish_out(b, j)

            batch(0, STEPS, True)
            with act.Fori(1, LAST - 1) as b:
                batch(b, STEPS)
            batch(LAST - 1, STEPS - 2)
            batch(LAST, 0)

        @block.vector
        def _(dve):
            def await_value(b, s):
                if s % G:
                    dve.wait_ge(y_ready, STEPS * b + s)
                    n = MASKS * b + s - s // G
                    dve.wait_ge(clamped, n)
                    dve.wait_ge(mask_ready, n)

            def select(s):
                if s % G:
                    nc.vector.copy_predicated(y[:, :], mask[:, s % MK, :].bitcast(i16), uq[:, s % 2, :]) \
                        .then_inc(y_ready, 1)

            def value(b, s):
                g = group_of(s)
                if s % G == 1:
                    dve.wait_ge(x1_ready, 2 * b + s // G)
                dve.wait_ge(t_ready, STEPS * b + s + 1)
                nc.vector.tensor_scalar(uq[:, s % 2, :], tq[:, s % TQ, :], -MAGIC, par[:, 1, g:g + 1],
                                        ALU.add, ALU.mult).then_inc(u_ready, 1)

            def clamp(b, s):
                g = group_of(s)
                dve.wait_ge(u_ready, STEPS * b + s + 1)
                clamped_y = uq[:, s % 2, :] if s % G else y[:, :]
                nc.vector.tensor_scalar(clamped_y, uq[:, s % 2, :], ylow[:, g:g + 1], yhigh[:, g:g + 1],
                                        ALU.max, ALU.min).then_inc(clamped if s % G else y_ready, 1)

            def cut_y(b, c):
                dve.wait_ge(y_ready, STEPS * b + G * (c + 1))
                nc.vector.scalar_tensor_tensor(ycut, absx[:, :], top[:, G - 1:G], y[:, :],
                                               ALU.is_gt, ALU.mult).then_inc(y_cut, 1)

            def add_y(b, c):
                dve.wait_ge(y_cut, 2 * b + c + 1)
                nc.vector.tensor_tensor(chunk(x1, c), chunk(xin, c), ycut, ALU.add).then_inc(x1_ready, 1)

            def quantiser(b, s, first=False, meanwhile=None):
                before = None if first and s == 0 else (b, s - 1) if s else (b - 1, STEPS - 1)
                if before:
                    await_value(*before)
                value(b, s)
                if meanwhile:
                    meanwhile()
                if before:
                    select(before[1])
                    if s % G == 0:
                        chunk_before = (before[0], before[1] // G)
                        cut_y(*chunk_before)
                        add_y(*chunk_before)
                        dve.wait_ge(y_cut, 2 * chunk_before[0] + chunk_before[1] + 1)
                clamp(b, s)

            def flush(b):
                await_value(b, STEPS - 1)
                select(STEPS - 1)
                cut_y(b, 1)
                add_y(b, 1)

            def finish_x2(b, j):
                dve.wait_ge(pair_done, 2 * PAIRS * b + j + 1)
                if j >= 2:
                    dve.wait_ge(x2l_ready, PAIRS * b + j - 1)
                nc.vector.tensor_tensor(x2[:, j % 2, :], x2_bank[j][:, :],
                                        x1[:, 2 * j:2 * j + 2, :].rearrange("p k t -> p (k t)"), ALU.add) \
                    .then_inc(x2_ready, 1)

            def split_x2(b, j):
                dve.wait_ge(x2h_ready, PAIRS * b + j + 1)
                pair = slice(2 * j, 2 * j + 2)
                nc.vector.tensor_tensor(x2l[:, pair, :].rearrange("p k t -> p (k t)"), x2[:, j % 2, :],
                                        x2h[:, pair, :].rearrange("p k t -> p (k t)").bitcast(f32),
                                        ALU.subtract).then_inc(x2l_ready, 1)

            def split_v(b):
                dve.wait_ge(vh_ready, 4 * (b + 1))
                for c in (0, DUP):
                    for src, lo, hi in ((va, c, c + R2), (vg, c + R2, c + R)):
                        nc.vector.tensor_tensor(vl[:, :, lo:hi], src[:, :, :], vh[:, :, lo:hi].bitcast(f32),
                                                ALU.subtract).then_inc(vl_ready, 1)

            def split_u(b):
                dve.wait_ge(uh_ready, b + 1)
                nc.vector.tensor_tensor(ul0[0:DUP, :], ua[0:DUP, :], uhh[0:DUP, :].bitcast(f32),
                                        ALU.subtract).then_inc(ul_ready, 1)

            def split_low(b):
                dve.wait_ge(lowh_ready, 2 * (b + 1))
                nc.vector.scalar_tensor_tensor(lows[DUP:P, :], low_bank[DUP:P, 0:T], lscale[DUP:P, 0:1],
                                               lowh[DUP:P, :].bitcast(f32), ALU.mult, ALU.subtract) \
                    .then_inc(lows_ready, 1)

            nc.vector.memset(magic[:, :], MAGIC).then_inc(pads, 1)
            dve.wait_ge(par_in, 16)
            nc.vector.max(top[:, :], par[:, 0, :]).then_inc(par_step, 1)
            nc.vector.reciprocal(rdelta[:, :], par[:, 1, :]).then_inc(par_step, 1)
            nc.vector.tensor_scalar(ylow[:, :], par[:, 2, :], -1.0, None, ALU.mult).then_inc(par_step, 1)
            nc.vector.tensor_scalar(yhigh[:, :], par[:, 2, :], -1.0, TOP_LEVEL, ALU.mult, ALU.add) \
                .then_inc(par_step, 1)
            dve.wait_ge(par_step, 4)
            nc.vector.tensor_scalar(negtop[:, :], top[:, :], -1.0, None, ALU.mult).then_inc(par_step, 1)
            nc.vector.tensor_tensor(ylow[:, :], ylow[:, :], par[:, 1, :], ALU.mult).then_inc(par_step, 1)
            nc.vector.tensor_tensor(yhigh[:, :], yhigh[:, :], par[:, 1, :], ALU.mult).then_inc(par_step, 1)
            nc.vector.memset(top_spare[:, 0:1], 0.0).then_inc(x2_ready, PAIRS)
            nc.vector.memset(top_spare[:, 1:2], 0.0).then_inc(out_ready, OUT_BANKS)
            dve.wait_ge(par_step, 7)

            def adapters_part(s):
                if s == 4:
                    dve.wait_ge(d_done, 1)
                    for a in range(NA):
                        nc.vector.tensor_scalar(dmask[:, a, :], de_bank[:, 0:R2], rows[:, a:a + 1], None,
                                                ALU.mult).then_inc(dmask_ready, 1)
                if s in (11, 14):
                    h = (s - 11) // 3
                    tiles = slice(h * HALF, (h + 1) * HALF)
                    dve.wait_ge(g_done, HALF * (h + 1))
                    for i in range(h * HALF, (h + 1) * HALF):
                        done = nc.vector.tensor_tensor(
                            gsb[:, :, i, :],
                            out_bank[h][:, (i % HALF) * P:(i % HALF + 1) * P].rearrange("p (a r) -> p a r", a=NA),
                            b3s[:, i, :].rearrange("p (a r) -> p a r", a=NA), ALU.add)
                    done.then_inc(g_ready, 1)
                if 6 <= s < 6 + 2 * EH:
                    e = s - 6
                    dve.wait_ge(e_done, e + 1)
                    if e >= 2:
                        dve.wait_ge(e_out[e % 2], 16)
                    nc.vector.tensor_tensor(esb[:, e % 2, :], de_bank[:, :],
                                            b2rep[:, (e % 2) * 512:(e % 2 + 1) * 512], ALU.add) \
                        .then_inc(e_ready, 1)

            for s in range(STEPS):
                quantiser(0, s, True)
                adapters_part(s)
            quantiser(1, 0)

            def batch(b, steps, early=False):
                v_at, u_at, low_at = at(early, 4, 5, 10)
                finish_at = at(early, 5, 6, 7, 8)
                for s in range(1, STEPS + 1):
                    if s == v_at:
                        split_v(b)
                    if s == u_at:
                        split_u(b)
                    if s == low_at:
                        split_low(b)
                    for j in range(PAIRS):
                        if s == finish_at[j]:
                            finish_x2(b, j)
                    urgent = (lambda: split_x2(b, PAIRS - 1)) if s == finish_at[-1] else None
                    if s < 1 + steps:
                        quantiser(b + 1 + s // STEPS, s % STEPS, meanwhile=urgent)
                    elif urgent:
                        urgent()
                    for j in range(PAIRS - 1):
                        if s == finish_at[j]:
                            split_x2(b, j)

            batch(0, STEPS, True)
            with dve.Fori(1, LAST - 1) as b:
                batch(b, STEPS)
            batch(LAST - 1, STEPS - 1)
            flush(LAST)
            batch(LAST, 0)

        @block.tensor
        def _(pe):
            pe.wait_ge(small_in, 96)
            for k in range(KT):
                last = nc.tensor.matmul(de_bank[:, 0:R2], b3s[:, k, :], b2s[:, k, :],
                                        start=(k == 0), stop=(k == KT - 1))
            last.then_inc(d_done, 1)

            def adapters_e(e):
                per = P // R2
                h, n = divmod(e, 2)
                if e:
                    pe.wait_ge(e_ready, e)
                else:
                    pe.wait_ge(dmask_ready, NA)
                nc.tensor.matmul(de_bank[:, :], dmask[:, h * per:(h + 1) * per, :].rearrange("p a r -> p (a r)"),
                                 a3s[:, n * 512:(n + 1) * 512], start=True, stop=True).then_inc(e_done, 1)

            for i in range(KT):
                pe.wait_ge(stage_in[i % 2], 16 * (i // 2 + 1))
                for o in range(OT):
                    last = nc.tensor.matmul(out_bank[i // HALF][:, (i % HALF) * P:(i % HALF + 1) * P],
                                            stage[:, i % 2, o * P:(o + 1) * P], b3s[:, o, :],
                                            start=(o == 0), stop=(o == OT - 1))
                last.then_inc(g_done, 1)
                e = i - HALF + 1
                if 0 <= e < 2 * EH:
                    adapters_e(e)

            def product(b, o, tiles):
                into = out_bank[o // 2 % OUT_BANKS][:, (o % 2) * T:(o % 2 + 1) * T]
                for k in tiles:
                    cut = slice(k * P, (k + 1) * P)
                    for i, (w, xs) in enumerate(((w2h, x2h), (w2l, x2h), (w2h, x2l))):
                        nc.tensor.matmul(into, w[:, o, cut], xs[:, k, :], start=(o % 2 == 0 and k == 0 and i == 0),
                                         stop=False, skip_group_check=True)

            def v_x2(tiles):
                for k in tiles:
                    for i, (v, xs) in enumerate(((vh, x2h), (vl, x2h), (vh, x2l))):
                        last = nc.tensor.matmul(low_bank[:, 0:T], v[:, k, :], xs[:, k, :],
                                                start=(k == 0 and i == 0), stop=(k == KT - 1 and i == 2),
                                                skip_group_check=True)
                return last

            def batch(b, w2_comes=False):
                for c in range(2):
                    pe.wait_ge(x1_ready, 2 * b + c + 1)
                    for o in range(OT):
                        j = o // 2
                        if c == 0 and o % 2 == 0:
                            pe.wait_ge(w1_in[j], 16 * (b + 1))
                            pe.wait_ge(x2_ready, PAIRS * b + j + 1)
                        for k in range(c * HALF, (c + 1) * HALF):
                            last = nc.tensor.matmul(x2_bank[j][:, (o % 2) * T:(o % 2 + 1) * T],
                                                    w1b[:, o, k * P:(k + 1) * P], x1[:, k, :],
                                                    start=(o % 2 == 0 and k == 0), stop=(k == KT - 1),
                                                    skip_group_check=True)
                        if c == 1 and o % 2 == 1:
                            last.then_inc(pair_done, 1)
                early, late = range(KT - 2), range(KT - 2, KT)
                pe.wait_ge(vl_ready, 4 * (b + 1))
                pe.wait_ge(x2l_ready, PAIRS * (b + 1) - 1)
                v_x2(early)
                pe.wait_ge(out_ready, PAIRS * b + 1)
                if w2_comes:
                    pe.wait_ge(w2l_ready, 1)
                product(b, 0, early)
                pe.wait_ge(x2l_ready, PAIRS * (b + 1))
                v_x2(late).then_inc(low_done, 1)
                product(b, 0, late)
                for o in range(1, OT):
                    if o % 2 == 0:
                        pe.wait_ge(out_ready, PAIRS * b + o // 2 + 1)
                    if w2_comes:
                        pe.wait_ge(w2l_ready, o + 1)
                    product(b, o, range(KT))
                    if o % 2 == 1:
                        if o == 1:
                            pe.wait_ge(lows_ready, b + 1)
                            pe.wait_ge(ul_ready, b + 1)
                        for q in (o - 1, o):
                            into = out_bank[o // 2 % OUT_BANKS][:, (q % 2) * T:(q % 2 + 1) * T]
                            cut = slice(q * P, (q + 1) * P)
                            nc.tensor.matmul(into, uhh[:, cut], lows[:, :], start=False, stop=False,
                                             skip_group_check=True)
                            last = nc.tensor.matmul(into, ul0[:, cut], lows[:, :], start=False, stop=True,
                                                    skip_group_check=True)
                        last.then_inc(pair_done, 1)

            pe.wait_ge(g_ready, 2)
            batch(0, True)
            with pe.Fori(1, B) as b:
                batch(b)


def kernel(**inputs):
    import numpy as np
    import concourse.bacc as bacc
    from concourse.bass_utils import run_bass_kernel_spmd

    P = 128
    x = np.asarray(inputs["x"])
    B, T, D = x.shape
    KT = D // P
    w1 = np.asarray(inputs["L1_cond_weight"])
    w2 = np.asarray(inputs["L2_cond_W"])
    la = np.asarray(inputs["L2_cond_lora_A"])
    b2 = np.asarray(inputs["L2_cond_lora_B_w"])
    a3 = np.asarray(inputs["L3_cond_A"])
    b3 = np.asarray(inputs["L3_cond_B"])
    NA, NL, R2, R3 = w1.shape[0], la.shape[0], la.shape[2], a3.shape[2]
    params = np.stack([np.asarray(inputs[n]) for n in
                       ("condB_thresholds", "condB_deltas", "condB_zeropoints")])
    row = np.arange(P)
    arrays = {
        "x": x.reshape(B, T, KT, P).transpose(0, 3, 2, 1),
        "params": np.broadcast_to(params, (P,) + params.shape),
        "w1": w1.reshape(NA, KT, P, KT, P).transpose(0, 4, 1, 3, 2).reshape(NA, P, KT, D),
        "w2t": w2.reshape(KT, P, KT, P).transpose(0, 3, 2, 1).reshape(KT, P, D),
        "w2n": w2.reshape(KT, P, KT, P).transpose(2, 1, 0, 3).reshape(KT, P, D),
        "b3t": b3.reshape(NA * R3, KT, P).transpose(2, 1, 0),
        "b2n": b2.reshape(KT, P, R2).transpose(1, 0, 2),
        "b2r": np.tile(b2.T, (P // R2, 1)),
        "a3": a3.transpose(0, 2, 1).reshape(NA * R3, D),
        "la": la.reshape(NL, KT, P, R2).transpose(0, 2, 1, 3),
        "ids_b": np.asarray(inputs["itok_B_0_2"]).reshape(1, B),
        "ids_a": np.asarray(inputs["itok_B_3_7"]).reshape(1, B),
        "own_rows": (row[:, None] // R3 == np.arange(NA)).astype(np.float32),
        "ident": np.eye(P, dtype=np.float32),
        "low_scale": np.where(row % 64 < R2, 0.5, 1.0).astype(np.float32)[:, None],
    }
    arrays = {n: np.ascontiguousarray(a) for n, a in arrays.items()}
    nc = bacc.Bacc("TRN2", target_bir_lowering=False, num_devices=1)
    args = {n: nc.dram_tensor(n, a.shape, mybir.dt.from_np(a.dtype), kind="ExternalInput").ap()
            for n, a in arrays.items()}
    args["out"] = nc.dram_tensor("out", (B, P, KT // 2, 2 * T), mybir.dt.float32, kind="ExternalOutput").ap()
    args["e_dram"] = nc.dram_tensor("e_dram", (NA, R2, D), mybir.dt.float32, kind="Internal").ap()
    args["g_dram"] = nc.dram_tensor("g_dram", (NA, P, KT, R3), mybir.dt.float32, kind="Internal").ap()
    quantised_residual_adapter_stack(nc, **args)
    r = run_bass_kernel_spmd(nc, [arrays], core_ids=[0])
    got = np.asarray(r.results[0]["out"]).reshape(B, P, KT, T)
    return np.ascontiguousarray(got.transpose(0, 3, 2, 1).reshape(B, T, D))
```

```python
import concourse.bass as bass
from concourse import mybir
from contextlib import ExitStack


def quantised_residual_adapter_stack(nc, x, params, w1, w2t, w2n, b3t, b2n, b2r, a3, la, ids_b, ids_a,
                                     own_rows, low_scale, ident, out, e_dram, g_dram):
    f32, f32r, bf16, i16 = mybir.dt.float32, mybir.dt.float32r, mybir.dt.bfloat16, mybir.dt.int16
    ALU = mybir.AluOpType
    ACT = mybir.ActivationFunctionType

    P = 128
    B, _, KT, T = x.shape
    OT = KT
    G = params.shape[2]
    NA = w1.shape[0]
    NL = la.shape[0]
    R2 = b2n.shape[2]
    R3 = a3.shape[0] // NA
    R = R2 + R3
    D = KT * P
    HALF = KT // 2
    CH = HALF * T
    TOP_LEVEL = 63.0
    MAGIC = 1.5 * 2.0 ** 23
    PAIRS = OT // 2
    OUT_BANKS = 2
    STEPS = 2 * G
    MASKS = STEPS - 2
    DUP = 64
    EH = NA * R2 // P
    LAST = B - 1
    TQ, MK = 4, 2

    ctx = ExitStack()
    with ctx:
        def sb(name, shape, dt=f32):
            return ctx.enter_context(nc.sbuf_tensor(name, shape, dt))

        def pb(name):
            return ctx.enter_context(nc.psum_tensor(name, [P, 512], f32))

        def sem(name):
            return ctx.enter_context(nc.semaphore(name))

        def chunk(t, c):
            return t[:, c * HALF:(c + 1) * HALF, :].rearrange("p k t -> p (k t)")

        xin = sb("xin", [P, KT, T])
        x1 = sb("x1", [P, KT, T])
        x2 = sb("x2", [P, 2, 2 * T])
        x2h = sb("x2h", [P, KT, T], f32r)
        x2l = sb("x2l", [P, KT, T], f32r)
        outb = sb("outb", [P, PAIRS, 2 * T])
        w1b = sb("w1b", [P, OT, KT * P])
        w2h = sb("w2h", [P, OT, KT * P], f32r)
        w2l = sb("w2l", [P, OT, KT * P], f32r)
        stage = sb("stage", [P, 2, KT * P])
        absx = sb("absx", [P, CH])
        tq = sb("tq", [P, TQ, CH])
        uq = sb("uq", [P, 2, CH])
        mask = sb("mask", [P, MK, CH], bf16)
        y = sb("y", [P, CH])
        par = sb("par", [P, 3, G])
        top = sb("top", [P, 8])
        negtop = sb("negtop", [P, 8])
        rdelta = sb("rdelta", [P, G])
        ylow = sb("ylow", [P, G])
        yhigh = sb("yhigh", [P, G])
        magic = sb("magic", [P, 1])
        scrap = sb("scrap", [P, 2])
        lscale = sb("lscale", [P, 1])
        ua = sb("ua", [P, D])
        uhh = sb("uhh", [P, D], f32r)
        ul0 = sb("ul0", [P, D], f32r)
        va = sb("va", [P, KT, R2])
        vg = sb("vg", [P, KT, R3])
        vh = sb("vh", [P, KT, P], f32r)
        vl = sb("vl", [P, KT, P], f32r)
        lowh = sb("lowh", [P, T], f32r)
        lows = sb("lows", [P, T], f32r)
        ycut = uq[:, 1, :]
        b3s = chunk(x1, 1).rearrange("p (k r) -> p k r", k=KT)
        a3s = outb[:, 0:2, :].rearrange("p j t -> p (j t)")
        b2s = outb[:, 2, 0:KT * R2].rearrange("p (k r) -> p k r", k=KT)
        dmask = outb[:, 2, KT * R2:KT * R2 + NA * R2].rearrange("p (a r) -> p a r", a=NA)
        eye = outb[:, 3, 0:P]
        rows = outb[:, 3, P:P + NA]
        gsb = ua[:, :].rearrange("p (a k r) -> p a k r", a=NA, k=KT)
        b2rep = x2[:, :, :].rearrange("p j t -> p (j t)")
        w2g = w1b
        e_place = [outb[:, 0, :], outb[:, 1, :], outb[:, 2, :], x2[:, 1, :]]

        x2_bank = [pb(f"x2_bank{i}") for i in range(PAIRS)]
        out_bank = [pb(f"out_bank{i}") for i in range(OUT_BANKS)]
        low_bank = pb("low_bank")
        de_bank = pb("de_bank")
        e_bank = [low_bank, de_bank] + out_bank

        par_in = sem("par_in")
        x_in = [sem(f"x_in{c}") for c in range(2)]
        w1_in = [sem(f"w1_in{j}") for j in range(PAIRS)]
        b_in = sem("b_in")
        small_in = sem("small_in")
        w2g_in = [sem(f"w2g_in{j}") for j in range(KT // 2)]
        stage_in = [sem(f"stage_in{c}") for c in range(2)]
        u_in = sem("u_in")
        v_in = sem("v_in")
        store_done = [sem(f"store_done{c}") for c in range(2)]
        pads = sem("pads")
        ua_zero = sem("ua_zero")
        par_step = sem("par_step")
        negtop_ready = sem("negtop_ready")
        abs_ready = sem("abs_ready")
        t_ready = sem("t_ready")
        mask_ready = sem("mask_ready")
        u_ready = sem("u_ready")
        clamped = sem("clamped")
        y_ready = sem("y_ready")
        y_cut = sem("y_cut")
        x1_ready = sem("x1_ready")
        pair_done = sem("pair_done")
        x2_ready = sem("x2_ready")
        out_ready = sem("out_ready")
        e_out = sem("e_out")
        diag_ready = sem("diag_ready")
        x2h_ready = sem("x2h_ready")
        x2l_ready = sem("x2l_ready")
        vh_ready = sem("vh_ready")
        vl_ready = sem("vl_ready")
        uh_ready = sem("uh_ready")
        ul_ready = sem("ul_ready")
        low_done = sem("low_done")
        lowh_ready = sem("lowh_ready")
        lows_ready = sem("lows_ready")
        d_done = sem("d_done")
        dmask_ready = sem("dmask_ready")
        g_tiles = sem("g_tiles")
        g_ready = sem("g_ready")
        e_done = sem("e_done")
        e_ready = sem("e_ready")
        w2h_ready = sem("w2h_ready")
        w2l_ready = sem("w2l_ready")

        block = ctx.enter_context(nc.Block())

        def group_of(s):
            return G - 1 - s % G

        def selections(b, s):
            return MASKS * b + s - s // G

        def x2_pairs(n):
            return PAIRS + n

        def out_pairs(n):
            return OUT_BANKS + n

        @block.sync
        def _(sp):
            def load_x(b, c):
                cut = slice(c * HALF, (c + 1) * HALF)
                sp.dma_start(xin[:, cut, :], x[bass.ds(b, 1), :, cut, :].rearrange("b p k t -> (b p) k t")) \
                    .then_inc(x_in[c], 16)

            def load_w1(a, j):
                sp.dma_start(w1b[:, 2 * j:2 * j + 2, :],
                             w1[bass.ds(a, 1), :, 2 * j:2 * j + 2, :].rearrange("a p j n -> (a p) j n")) \
                    .then_inc(w1_in[j], 16)

            def load_u(a):
                for r in (0, DUP):
                    sp.dma_start(ua[r:r + R2, :], e_dram[bass.ds(a, 1)].rearrange("a r n -> (a r) n")) \
                        .then_inc(u_in, 16)
                    sp.dma_start(ua[r + R2:r + R, :], a3[bass.ds(a * R3, R3), :]).then_inc(u_in, 16)

            def load_v(a, lab):
                sp.dma_start(va[:, :, :], la[bass.ds(lab, 1)].rearrange("a p k r -> (a p) k r")) \
                    .then_inc(v_in, 16)
                sp.dma_start(vg[:, :, :], g_dram[bass.ds(a, 1)].rearrange("a p k r -> (a p) k r")) \
                    .then_inc(v_in, 16)

            def ids_of(b):
                a = sp.value_load(ids_a[0:1, bass.ds(b, 1)], min_val=0, max_val=NA - 1)
                lab = sp.value_load(ids_b[0:1, bass.ds(b, 1)], min_val=0, max_val=NL - 1)
                return a, lab

            def store(b, c):
                sp.dma_start(out[bass.ds(b, 1), :, 2 * c:2 * c + 2, :].rearrange("b p j t -> (b p) j t"),
                             outb[:, 2 * c:2 * c + 2, :]).then_inc(store_done[c], 16)

            def load_w2g(i):
                sp.dma_start(w2g[:, i:i + 2, :], w2n[i:i + 2].rearrange("i p n -> p i n")).then_inc(w2g_in[i // 2], 16)

            sp.dma_start(par[:, :, :], params[:, :, :]).then_inc(par_in, 16)
            load_x(0, 0)
            for dst, src in ((b3s, b3t), (b2s, b2n), (eye, ident), (rows, own_rows)):
                sp.dma_start(dst, src).then_inc(b_in, 16)
            load_x(0, 1)
            load_w2g(0)
            for dst, src in ((lscale[:, :], low_scale), (a3s, a3), (b2rep, b2r)):
                sp.dma_start(dst, src).then_inc(small_in, 16)
            for i in range(2, KT, 2):
                load_w2g(i)
            a0, lab0 = ids_of(0)

            def store_e(e, done):
                h, n = divmod(e, 2)
                sp.wait_ge(e_ready, e + 1)
                sp.dma_start(e_dram.rearrange("(h a) r n -> h (a r) n", h=EH)[h, :, n * 512:(n + 1) * 512],
                             e_place[e]).then_inc(done, 16)

            def load_w2(i):
                sp.dma_start(stage[:, i % 2, :], w2t[i, :, :]).then_inc(stage_in[i % 2], 16)

            load_w2(0)
            load_w2(1)
            for j in range(PAIRS):
                sp.wait_ge(g_tiles, 2 * (j + 1))
                load_w1(a0, j)
            sp.wait_ge(g_ready, 2)
            sp.dma_start(g_dram.rearrange("a p k r -> p a k r"), gsb[:, :, :, :]).then_inc(store_done[0], 16)
            sp.wait_ge(x1_ready, 1)
            load_x(1, 0)
            sp.wait_ge(store_done[0], 16)
            load_v(a0, lab0)
            E_AFTER = (3, 3, 4, 4)
            for i in range(2, OT):
                if i == OT // 2:
                    sp.wait_ge(x1_ready, 2)
                    load_x(1, 1)
                sp.wait_ge(w2l_ready, i - 1)
                load_w2(i)
                for e in range(2 * EH):
                    if i == E_AFTER[e]:
                        store_e(e, e_out if e < 2 * EH - 1 else store_done[1])
                if i == E_AFTER[-1] + 1:
                    sp.wait_ge(store_done[1], 16)
                    sp.wait_ge(e_out, 16 * (2 * EH - 1))
                    sp.wait_ge(ua_zero, 1)
                    load_u(a0)

            def next_batch(b, ahead):
                a, lab = ids_of(b + 1)
                for j in range(PAIRS):
                    sp.wait_ge(pair_done, 2 * PAIRS * b + j + 1)
                    load_w1(a, j)
                if ahead:
                    sp.wait_ge(x1_ready, 2 * (b + 1) + 1)
                    load_x(b + 2, 0)
                sp.wait_ge(vl_ready, 4 * (b + 1))
                sp.wait_ge(ul_ready, b + 1)
                load_v(a, lab)
                load_u(a)
                for c in range(2):
                    sp.wait_ge(out_ready, out_pairs(PAIRS * b + 2 * c + 2))
                    store(b, c)
                if ahead:
                    sp.wait_ge(x1_ready, 2 * (b + 1) + 2)
                    load_x(b + 2, 1)

            with sp.Fori(0, LAST - 1) as b:
                next_batch(b, True)
            next_batch(LAST - 1, False)
            for j in range(PAIRS):
                sp.wait_ge(out_ready, out_pairs(PAIRS * LAST + j + 1))
                sp.dma_start(out[LAST, :, j, :], outb[:, j, :]).then_inc(store_done[j // 2], 16)
            for c in range(2):
                sp.wait_ge(store_done[c], 16 * (B + 2))

        @block.gpsimd
        def _(pool):
            nc.gpsimd.memset(vh[:, :, :].bitcast(f32), 0.0).then_inc(pads, 1)
            nc.gpsimd.memset(vl[:, :, :].bitcast(f32), 0.0).then_inc(pads, 1)
            nc.gpsimd.memset(ul0[:, :].bitcast(f32), 0.0).then_inc(pads, 1)
            pool.wait_ge(b_in, 64)
            for o in range(OT):
                pool.wait_ge(stage_in[o % 2], 16 * (o // 2 + 1))
                diag = stage[:, o % 2, o * P:(o + 1) * P]
                nc.gpsimd.tensor_tensor(diag, diag, eye, ALU.add).then_inc(diag_ready, 1)
                pool.wait_ge(w2h_ready, o + 1)
                nc.gpsimd.tensor_tensor(w2l[:, o, :], stage[:, o % 2, :], w2h[:, o, :].bitcast(f32),
                                        ALU.subtract).then_inc(w2l_ready, 1)
                if o == 1:
                    pool.wait_ge(store_done[0], 16)
                    nc.gpsimd.memset(ua[:, :], 0.0).then_inc(ua_zero, 1)

        D_AT, G_AT = 9, (10, 12)
        E_AT = (STEPS + 2, STEPS + 2, STEPS + 3, STEPS + 3)
        W2_AT = (11, 14, 16, 17, STEPS + 5, STEPS + 6, STEPS + 7, STEPS + 9)
        FIRST, SECOND, THIRD, LATER = range(4)
        ACT_V, DVE_V = 2, 3
        ACT_U, DVE_U = (7, 4, 4, 4), (8, 5, 5, 5)
        ACT_X2 = ((4, 5, 6, 7), (6, 7, 8, 9), (7, 8, 9, 10), (8, 9, 10, 10))
        DVE_X2 = ((4, 5, 6, 7), (5, 6, 7, 8), (6, 7, 8, 9), (7, 8, 9, 9))
        ACT_LOW, DVE_LOW = (8, 10, 11, 12), (9, 9, 11, 12)
        ACT_OUT = ((10, 12, STEPS + 3, STEPS + 5), (12, 13, STEPS + 3, STEPS + 5),
                   (13, 14, STEPS + 3, STEPS + 5), (14, 15, STEPS + 3, STEPS + 5))

        @block.scalar
        def _(act):
            def multiple(b, s, first=False):
                c, g = s // G, group_of(s)
                if s % G == 0:
                    act.wait_ge(x_in[c], 16 * (b + 1))
                if not (first and s < TQ):
                    act.wait_ge(clamped, STEPS * b + s - TQ + 1)
                nc.scalar.activation(tq[:, s % TQ, :], chunk(xin, c), ACT.Identity, bias=magic[:, 0:1],
                                     scale=rdelta[:, g:g + 1]).then_inc(t_ready, 1)

            def exceeds(b, s, first=False):
                c, g = s // G, group_of(s)
                if s % G == 1:
                    if not (first and c == 0):
                        act.wait_ge(y_cut, 2 * b + c)
                    nc.scalar.activation(absx[:, :], chunk(xin, c), ACT.Abs).then_inc(abs_ready, 1)
                    act.wait_ge(abs_ready, 2 * b + c + 1)
                if s % G:
                    if first and s == 1:
                        act.wait_ge(negtop_ready, 1)
                    if not (first and s <= MK):
                        act.wait_ge(y_ready, selections(b, s - MK))
                    nc.scalar.activation(mask[:, s % MK, :], absx[:, :], ACT.Relu,
                                         bias=negtop[:, g:g + 1], scale=1.0).then_inc(mask_ready, 1)

            def quantiser(b, s, first=False):
                multiple(b, s, first)
                if s >= 2:
                    exceeds(b, s - 2, first)
                elif not first:
                    exceeds(b - 1, s - 2 + STEPS)

            def round_x2(b, j):
                act.wait_ge(x2_ready, x2_pairs(PAIRS * b + j + 1))
                nc.scalar.activation(x2h[:, 2 * j:2 * j + 2, :].rearrange("p k t -> p (k t)"),
                                     x2[:, j % 2, :], ACT.Copy).then_inc(x2h_ready, 1)

            def round_v(b, first):
                act.wait_ge(v_in, 32 * (b + 1))
                if not first:
                    act.wait_ge(low_done, b)
                for c in (0, DUP):
                    nc.scalar.activation(vh[:, :, c:c + R2], va[:, :, :], ACT.Copy).then_inc(vh_ready, 1)
                    nc.scalar.activation(vh[:, :, c + R2:c + R], vg[:, :, :], ACT.Copy).then_inc(vh_ready, 1)

            def round_u(b, first):
                act.wait_ge(u_in, 64 * (b + 1))
                if not first:
                    act.wait_ge(pair_done, 2 * PAIRS * b)
                nc.scalar.activation(uhh[:, :], ua[:, :], ACT.Copy).then_inc(uh_ready, 1)

            def round_low(b):
                act.wait_ge(low_done, b + 1)
                nc.scalar.activation(lowh[:, :], low_bank[:, 0:T], ACT.Copy, scale=lscale[:, 0:1]) \
                    .then_inc(lowh_ready, 1)
                nc.scalar.activation(lows[0:DUP, :], low_bank[0:DUP, 0:T], ACT.Copy,
                                     scale=lscale[0:DUP, 0:1]).then_inc(lowh_ready, 1)

            def round_w2(o):
                act.wait_ge(diag_ready, o + 1)
                nc.scalar.activation(w2h[:, o, :], stage[:, o % 2, :], ACT.Copy).then_inc(w2h_ready, 1)

            def finish_out(b, j):
                if j % 2 == 0:
                    act.wait_ge(store_done[j // 2], 16 * (b + 1))
                act.wait_ge(pair_done, 2 * PAIRS * b + PAIRS + j + 1)
                nc.scalar.activation(outb[:, j, :], out_bank[j % OUT_BANKS][:, :], ACT.Copy) \
                    .then_inc(out_ready, 1)

            def adapters_part(s):
                if s == D_AT:
                    act.wait_ge(b_in, 64)
                    act.wait_ge(d_done, 1)
                    for a in range(NA):
                        nc.scalar.activation(dmask[:, a, :], de_bank[:, 0:R2], ACT.Copy,
                                             scale=rows[:, a:a + 1]).then_inc(dmask_ready, 1)
                for h in range(2):
                    if s == G_AT[h]:
                        act.wait_ge(g_tiles, HALF * (h + 1))
                        nc.scalar.activation(gsb[:, :, h * HALF:(h + 1) * HALF, :],
                                             out_bank[h][:, :].rearrange("p (i a r) -> p a i r", i=HALF, a=NA),
                                             ACT.Copy).then_inc(g_ready, 1)
                w2_and_e(s)

            def w2_and_e(s):
                for e in range(2 * EH):
                    if s == E_AT[e]:
                        act.wait_ge(e_done, 2 * EH)
                        nc.scalar.activation(e_place[e], e_bank[e][:, :], ACT.Copy).then_inc(e_ready, 1)
                for o in range(OT):
                    if s == W2_AT[o]:
                        round_w2(o)

            act.wait_ge(par_step, 1)
            nc.scalar.activation(negtop[:, :], top[:, :], ACT.Copy, scale=-1.0).then_inc(negtop_ready, 1)
            act.wait_ge(par_step, 6)
            for s in range(STEPS):
                quantiser(0, s, True)
                adapters_part(s)
            quantiser(1, 0)
            w2_and_e(STEPS)
            quantiser(1, 1)
            w2_and_e(STEPS + 1)
            act.wait_ge(pads, 4)

            def batch(b, slots, kind=LATER, before=LATER):
                for s in range(2, STEPS + 2):
                    if s < 2 + slots:
                        quantiser(b + 1 + s // STEPS, s % STEPS)
                    elif slots:
                        exceeds(b + 1, s - 2)
                    if s == ACT_V:
                        round_v(b, kind == FIRST)
                    for j in range(PAIRS):
                        if s == ACT_X2[kind][j]:
                            round_x2(b, j)
                    if s == ACT_U[kind]:
                        round_u(b, kind == FIRST)
                    if s == ACT_LOW[kind]:
                        round_low(b)
                    if kind == FIRST:
                        w2_and_e(STEPS + s)
                    for j in range(PAIRS):
                        if s == ACT_OUT[kind][j]:
                            finish_out(b, j)
                        elif kind != FIRST and s == ACT_OUT[before][j] - STEPS:
                            finish_out(b - 1, j)

            batch(0, STEPS, FIRST)
            batch(1, STEPS, SECOND, FIRST)
            batch(2, STEPS, THIRD)
            with act.Fori(3, LAST - 1) as b:
                batch(b, STEPS)
            batch(LAST - 1, STEPS - 2)
            batch(LAST, 0)
            finish_out(LAST, PAIRS - 2)
            finish_out(LAST, PAIRS - 1)

        @block.vector
        def _(dve):
            def value(b, s):
                g = group_of(s)
                dve.wait_ge(t_ready, STEPS * b + s + 1)
                nc.vector.tensor_scalar(tq[:, s % TQ, :], tq[:, s % TQ, :], -MAGIC, par[:, 1, g:g + 1],
                                        ALU.add, ALU.mult).then_inc(u_ready, 1)

            def clamp(b, s, first=False):
                g = group_of(s)
                dve.wait_ge(u_ready, STEPS * b + s + 1)
                if s % G == 1 and not (first and s == 1):
                    dve.wait_ge(x1_ready, 2 * b + s // G)
                clamped_y = uq[:, s % 2, :] if s % G else y[:, :]
                nc.vector.tensor_scalar(clamped_y, tq[:, s % TQ, :], ylow[:, g:g + 1], yhigh[:, g:g + 1],
                                        ALU.max, ALU.min).then_inc(clamped, 1)

            def await_selection(b, s, first=False):
                if s % G:
                    dve.wait_ge(clamped, STEPS * b + s + 1)
                    dve.wait_ge(mask_ready, selections(b, s))
                    if not (first and s == 1):
                        dve.wait_ge(y_ready, selections(b, s - 1))

            def select(s):
                if s % G:
                    nc.vector.copy_predicated(y[:, :], mask[:, s % MK, :].bitcast(i16), uq[:, s % 2, :]) \
                        .then_inc(y_ready, 1)

            def cut_y(b, c):
                dve.wait_ge(y_ready, selections(b, G * (c + 1) - 1))
                nc.vector.scalar_tensor_tensor(ycut, absx[:, :], top[:, G - 1:G], y[:, :],
                                               ALU.is_gt, ALU.mult).then_inc(y_cut, 1)

            def add_y(b, c):
                dve.wait_ge(y_cut, 2 * b + c + 1)
                nc.vector.tensor_tensor(chunk(x1, c), chunk(xin, c), ycut, ALU.add).then_inc(x1_ready, 1)

            def quantiser(b, s, first=False, meanwhile=None, after_select=None, before_add=None):
                def back(n):
                    return (b, s - n) if s >= n else None if first else (b - 1, s - n + STEPS)

                to_clamp, to_select = back(1), back(2)
                ends_chunk = s % G == 1 and to_select is not None
                if ends_chunk and not meanwhile:
                    await_selection(*to_select, first)
                value(b, s)
                if ends_chunk and meanwhile:
                    await_selection(*to_select, first)
                    meanwhile()
                if to_select and not ends_chunk:
                    await_selection(*to_select, first)
                if to_clamp and not ends_chunk:
                    clamp(*to_clamp, first)
                    if meanwhile:
                        meanwhile()
                if to_select:
                    select(to_select[1])
                if after_select:
                    after_select()
                if ends_chunk:
                    chunk_before = (to_select[0], to_select[1] // G)
                    cut_y(*chunk_before)
                    dve.wait_ge(y_cut, 2 * chunk_before[0] + chunk_before[1] + 1)
                    clamp(*to_clamp)
                    if before_add:
                        before_add()
                    add_y(*chunk_before)

            def flush(b):
                await_selection(b, STEPS - 2)
                clamp(b, STEPS - 1)
                select(STEPS - 2)
                await_selection(b, STEPS - 1)
                select(STEPS - 1)
                cut_y(b, 1)
                add_y(b, 1)

            def finish_x2(b, j, first=False):
                dve.wait_ge(pair_done, 2 * PAIRS * b + j + 1)
                if first and j == 1:
                    dve.wait_ge(store_done[1], 16)
                if j >= 2:
                    dve.wait_ge(x2l_ready, PAIRS * b + j - 1)
                nc.vector.tensor_tensor(x2[:, j % 2, :], x2_bank[j][:, :],
                                        x1[:, 2 * j:2 * j + 2, :].rearrange("p k t -> p (k t)"), ALU.add) \
                    .then_inc(x2_ready, 1)

            def split_x2(b, j):
                dve.wait_ge(x2h_ready, PAIRS * b + j + 1)
                pair = slice(2 * j, 2 * j + 2)
                nc.vector.tensor_tensor(x2l[:, pair, :].rearrange("p k t -> p (k t)"), x2[:, j % 2, :],
                                        x2h[:, pair, :].rearrange("p k t -> p (k t)").bitcast(f32),
                                        ALU.subtract).then_inc(x2l_ready, 1)

            def split_v(b):
                dve.wait_ge(vh_ready, 4 * (b + 1))
                for c in (0, DUP):
                    for src, lo, hi in ((va, c, c + R2), (vg, c + R2, c + R)):
                        nc.vector.tensor_tensor(vl[:, :, lo:hi], src[:, :, :], vh[:, :, lo:hi].bitcast(f32),
                                                ALU.subtract).then_inc(vl_ready, 1)

            def split_u(b):
                dve.wait_ge(uh_ready, b + 1)
                nc.vector.tensor_tensor(ul0[0:DUP, :], ua[0:DUP, :], uhh[0:DUP, :].bitcast(f32),
                                        ALU.subtract).then_inc(ul_ready, 1)

            def split_low(b):
                dve.wait_ge(lowh_ready, 2 * (b + 1))
                nc.vector.scalar_tensor_tensor(lows[DUP:P, :], low_bank[DUP:P, 0:T], lscale[DUP:P, 0:1],
                                               lowh[DUP:P, :].bitcast(f32), ALU.mult, ALU.subtract) \
                    .then_inc(lows_ready, 1)

            nc.vector.memset(magic[:, :], MAGIC).then_inc(pads, 1)
            dve.wait_ge(par_in, 16)
            nc.vector.max(top[:, :], par[:, 0, :]).then_inc(par_step, 1)
            nc.vector.reciprocal(rdelta[:, :], par[:, 1, :]).then_inc(par_step, 1)
            nc.vector.tensor_scalar(ylow[:, :], par[:, 2, :], -1.0, None, ALU.mult).then_inc(par_step, 1)
            nc.vector.tensor_scalar(yhigh[:, :], par[:, 2, :], -1.0, TOP_LEVEL, ALU.mult, ALU.add) \
                .then_inc(par_step, 1)
            dve.wait_ge(par_step, 4)
            nc.vector.tensor_tensor(ylow[:, :], ylow[:, :], par[:, 1, :], ALU.mult).then_inc(par_step, 1)
            nc.vector.tensor_tensor(yhigh[:, :], yhigh[:, :], par[:, 1, :], ALU.mult).then_inc(par_step, 1)
            nc.vector.memset(scrap[:, 0:1], 0.0).then_inc(x2_ready, PAIRS)
            nc.vector.memset(scrap[:, 1:2], 0.0).then_inc(out_ready, OUT_BANKS)
            dve.wait_ge(par_step, 6)

            for s in range(STEPS):
                quantiser(0, s, True)
            quantiser(1, 0)

            def batch(b, steps, kind=LATER):
                for s in range(1, STEPS + 1):
                    if s == DVE_V:
                        split_v(b)
                    if s == DVE_U[kind]:
                        split_u(b)
                    low = s == DVE_LOW[kind]
                    if low and kind != SECOND:
                        split_low(b)
                    pairs = [j for j in range(PAIRS) if s == DVE_X2[kind][j]]
                    if s < 1 + steps:
                        extras = {"before_add": lambda: split_low(b)} if low and kind == SECOND else {}
                        if pairs:
                            finish_x2(b, pairs[0], kind == FIRST)
                            extras["meanwhile"] = lambda: split_x2(b, pairs[0])
                        if len(pairs) == 2:
                            extras["after_select"] = lambda: finish_x2(b, pairs[1])
                            extras["before_add"] = lambda: split_x2(b, pairs[1])
                        quantiser(b + 1 + s // STEPS, s % STEPS, **extras)
                    else:
                        for j in pairs:
                            finish_x2(b, j)
                            split_x2(b, j)

            batch(0, STEPS, FIRST)
            batch(1, STEPS, SECOND)
            batch(2, STEPS, THIRD)
            with dve.Fori(3, LAST - 1) as b:
                batch(b, STEPS)
            batch(LAST - 1, STEPS - 1)
            flush(LAST)
            batch(LAST, 0)

        @block.tensor
        def _(pe):
            pe.wait_ge(b_in, 64)
            for k in range(KT):
                last = nc.tensor.matmul(de_bank[:, 0:R2], b3s[:, k, :], b2s[:, k, :],
                                        start=(k == 0), stop=(k == KT - 1))
            last.then_inc(d_done, 1)

            def adapters_e(e):
                per = P // R2
                h, n = divmod(e, 2)
                half = slice(n * 512, (n + 1) * 512)
                nc.tensor.matmul(e_bank[e][:, :], eye, b2rep[:, half], start=True, stop=False)
                nc.tensor.matmul(e_bank[e][:, :], dmask[:, h * per:(h + 1) * per, :].rearrange("p a r -> p (a r)"),
                                 a3s[:, half], start=False, stop=True).then_inc(e_done, 1)

            for i in range(KT):
                if i % 2 == 0:
                    pe.wait_ge(w2g_in[i // 2], 16)
                into = out_bank[i // HALF][:, (i % HALF) * P:(i % HALF + 1) * P]
                nc.tensor.matmul(into, eye, b3s[:, i, :], start=True, stop=False)
                for o in range(OT):
                    last = nc.tensor.matmul(into, w2g[:, i, o * P:(o + 1) * P], b3s[:, o, :],
                                            start=False, stop=(o == OT - 1))
                last.then_inc(g_tiles, 1)

            def product(o, tiles):
                into = out_bank[o // 2 % OUT_BANKS][:, (o % 2) * T:(o % 2 + 1) * T]
                for k in tiles:
                    cut = slice(k * P, (k + 1) * P)
                    for i, (w, xs) in enumerate(((w2h, x2h), (w2l, x2h), (w2h, x2l))):
                        nc.tensor.matmul(into, w[:, o, cut], xs[:, k, :], start=(o % 2 == 0 and k == 0 and i == 0),
                                         stop=False, skip_group_check=True)

            def v_x2(tiles):
                for k in tiles:
                    for i, (v, xs) in enumerate(((vh, x2h), (vl, x2h), (vh, x2l))):
                        last = nc.tensor.matmul(low_bank[:, 0:T], v[:, k, :], xs[:, k, :],
                                                start=(k == 0 and i == 0), stop=(k == KT - 1 and i == 2),
                                                skip_group_check=True)
                if tiles[-1] == KT - 1:
                    last.then_inc(low_done, 1)

            def u_low(j):
                for q in (2 * j, 2 * j + 1):
                    into = out_bank[j % OUT_BANKS][:, (q % 2) * T:(q % 2 + 1) * T]
                    cut = slice(q * P, (q + 1) * P)
                    nc.tensor.matmul(into, uhh[:, cut], lows[:, :], start=False, stop=False, skip_group_check=True)
                    last = nc.tensor.matmul(into, ul0[:, cut], lows[:, :], start=False, stop=True,
                                            skip_group_check=True)
                last.then_inc(pair_done, 1)

            def batch(b, w2_comes=False):
                for c in range(2):
                    pe.wait_ge(x1_ready, 2 * b + c + 1)
                    for o in range(OT):
                        j = o // 2
                        if c == 0 and o % 2 == 0:
                            pe.wait_ge(w1_in[j], 16 * (b + 1))
                            pe.wait_ge(x2_ready, PAIRS * b + j + 1)
                        for k in range(c * HALF, (c + 1) * HALF):
                            last = nc.tensor.matmul(x2_bank[j][:, (o % 2) * T:(o % 2 + 1) * T],
                                                    w1b[:, o, k * P:(k + 1) * P], x1[:, k, :],
                                                    start=(o % 2 == 0 and k == 0), stop=(k == KT - 1),
                                                    skip_group_check=True)
                        if c == 1 and o % 2 == 1:
                            last.then_inc(pair_done, 1)
                    if w2_comes and c == 0:
                        pe.wait_ge(dmask_ready, NA)
                        pe.wait_ge(small_in, 48)
                        pe.wait_ge(g_ready, 2)
                        for e in range(2 * EH):
                            adapters_e(e)
                pe.wait_ge(vl_ready, 4 * (b + 1))
                if w2_comes:
                    pe.wait_ge(e_ready, 2 * EH)
                for pairs in (range(PAIRS - 2), range(PAIRS - 2, PAIRS - 1), range(PAIRS - 1, PAIRS)):
                    tiles = range(2 * pairs[0], 2 * pairs[-1] + 2)
                    pe.wait_ge(x2l_ready, PAIRS * b + pairs[-1] + 1)
                    v_x2(tiles)
                    if pairs[0] == 0:
                        pe.wait_ge(out_ready, PAIRS * b + 1)
                    for o in range(2):
                        if w2_comes:
                            pe.wait_ge(w2l_ready, o + 1)
                        product(o, tiles)
                for o in range(2, OT):
                    if o % 2 == 0:
                        pe.wait_ge(out_ready, PAIRS * b + o // 2 + 1)
                    if w2_comes:
                        pe.wait_ge(w2l_ready, o + 1)
                    product(o, range(KT))
                    if o == 2:
                        pe.wait_ge(lows_ready, b + 1)
                        pe.wait_ge(ul_ready, b + 1)
                        u_low(0)
                    elif o % 2 == 1:
                        u_low(o // 2)

            batch(0, True)
            with pe.Fori(1, B) as b:
                batch(b)


def kernel(**inputs):
    import numpy as np
    import concourse.bacc as bacc
    from concourse.bass_utils import run_bass_kernel_spmd

    P = 128
    x = np.asarray(inputs["x"])
    B, T, D = x.shape
    KT = D // P
    w1 = np.asarray(inputs["L1_cond_weight"])
    w2 = np.asarray(inputs["L2_cond_W"])
    la = np.asarray(inputs["L2_cond_lora_A"])
    b2 = np.asarray(inputs["L2_cond_lora_B_w"])
    a3 = np.asarray(inputs["L3_cond_A"])
    b3 = np.asarray(inputs["L3_cond_B"])
    NA, NL, R2, R3 = w1.shape[0], la.shape[0], la.shape[2], a3.shape[2]
    params = np.stack([np.asarray(inputs[n]) for n in
                       ("condB_thresholds", "condB_deltas", "condB_zeropoints")])
    row = np.arange(P)
    arrays = {
        "x": x.reshape(B, T, KT, P).transpose(0, 3, 2, 1),
        "params": np.broadcast_to(params, (P,) + params.shape),
        "w1": w1.reshape(NA, KT, P, KT, P).transpose(0, 4, 1, 3, 2).reshape(NA, P, KT, D),
        "w2t": w2.reshape(KT, P, KT, P).transpose(0, 3, 2, 1).reshape(KT, P, D),
        "w2n": w2.reshape(KT, P, KT, P).transpose(2, 1, 0, 3).reshape(KT, P, D),
        "b3t": b3.reshape(NA * R3, KT, P).transpose(2, 1, 0),
        "b2n": b2.reshape(KT, P, R2).transpose(1, 0, 2),
        "b2r": np.tile(b2.T, (P // R2, 1)),
        "a3": a3.transpose(0, 2, 1).reshape(NA * R3, D),
        "la": la.reshape(NL, KT, P, R2).transpose(0, 2, 1, 3),
        "ids_b": np.asarray(inputs["itok_B_0_2"]).reshape(1, B),
        "ids_a": np.asarray(inputs["itok_B_3_7"]).reshape(1, B),
        "own_rows": (row[:, None] // R3 == np.arange(NA)).astype(np.float32),
        "ident": np.eye(P, dtype=np.float32),
        "low_scale": np.where(row % 64 < R2, 0.5, 1.0).astype(np.float32)[:, None],
    }
    arrays = {n: np.ascontiguousarray(a) for n, a in arrays.items()}
    nc = bacc.Bacc("TRN2", target_bir_lowering=False, num_devices=1)
    args = {n: nc.dram_tensor(n, a.shape, mybir.dt.from_np(a.dtype), kind="ExternalInput").ap()
            for n, a in arrays.items()}
    args["out"] = nc.dram_tensor("out", (B, P, KT // 2, 2 * T), mybir.dt.float32, kind="ExternalOutput").ap()
    args["e_dram"] = nc.dram_tensor("e_dram", (NA, R2, D), mybir.dt.float32, kind="Internal").ap()
    args["g_dram"] = nc.dram_tensor("g_dram", (NA, P, KT, R3), mybir.dt.float32, kind="Internal").ap()
    quantised_residual_adapter_stack(nc, **args)
    r = run_bass_kernel_spmd(nc, [arrays], core_ids=[0])
    got = np.asarray(r.results[0]["out"]).reshape(B, P, KT, T)
    return np.ascontiguousarray(got.transpose(0, 3, 2, 1).reshape(B, T, D))
```
